# Optimizing a Trainium2 kernel written in Bass

```python
import numpy as np
import jax
import jax.numpy as jnp

def _softmax(x, axis=-1):
    return jax.nn.softmax(x, axis=axis)

def _gelu(x):
    return jax.nn.gelu(x, approximate=True)

def _silu(x):
    return jax.nn.silu(x)

def _sigmoid(x):
    return jax.nn.sigmoid(x)

def _layernorm(x, axis=-1, eps=1e-05):
    m = jnp.mean(x, axis=axis, keepdims=True)
    v = jnp.var(x, axis=axis, keepdims=True)
    return (x - m) / jnp.sqrt(v + eps)

def _scatter_add(tgt, idx, src, axis=0):
    return tgt.at[idx].add(src)

def _segment_sum(src, seg, n):
    return jax.ops.segment_sum(src, seg, n)
kernel_name = 'mk_adaln_d1_jaxref_r8_eaa770'

def setup_inputs(seed: int=0):
    np.random.seed(seed)
    _w = jnp.asarray

    def _L0_attn_setup():
        import jax, jax.numpy as jnp
        import numpy as np
        EMBED = 128
        EXPAND = 128
        B, T = (4, 256)
        PI = 3.141592653589793
        EPS = 1e-05

        def _gla_scan(q, k, v, g):
            Bq, Tq, H, Dk = q.shape
            Dv = v.shape[-1]
            scale = Dk ** (-0.5)

            def step(S, inp):
                qt, kt, vt, gt = inp
                S = S * jnp.exp(gt)[..., None] + kt[..., None] * vt[..., None, :]
                o = jnp.einsum('bhk,bhkv->bhv', qt * scale, S)
                return (S, o)
            S0 = jnp.zeros((Bq, H, Dk, Dv), q.dtype)
            seq = tuple((jnp.moveaxis(a, 1, 0) for a in (q, k, v, g)))
            _, out = jax.lax.scan(step, S0, seq)
            return jnp.moveaxis(out, 0, 1)
        key = jax.random.key(seed)
        ks = jax.random.split(key, 8)
        std = 0.02
        return {'x': jax.random.normal(ks[0], (B, T, EMBED), jnp.float32), 'wq': jax.random.normal(ks[1], (EMBED, EMBED), jnp.float32) * std, 'wk': jax.random.normal(ks[2], (EMBED, EMBED), jnp.float32) * std, 'wv': jax.random.normal(ks[3], (EMBED, EMBED), jnp.float32) * std, 'wo': jax.random.normal(ks[4], (EMBED, EMBED), jnp.float32) * std, 'wg1': jax.random.normal(ks[5], (EMBED, EXPAND), jnp.float32) * std, 'wg2': jax.random.normal(ks[6], (EXPAND, EMBED), jnp.float32) * std, 'norm_w': jnp.ones((EMBED,), jnp.float32)}
    _L0_attn_in = _L0_attn_setup()

    def _L0_ffn_setup():
        import jax, jax.numpy as jnp
        import numpy as np
        E = 8
        D = 128
        H = 256
        TOP_K = 2
        key = jax.random.key(seed)
        k_x, k_g, k_w1, k_w2 = jax.random.split(key, 4)
        B, S = (4, 256)
        inp = {'input': jax.random.normal(k_x, (B, S, D), dtype=jnp.float32), 'Wg': jax.random.normal(k_g, (D, E), dtype=jnp.float32) * 0.02, 'W1': jax.random.normal(k_w1, (E, D, H), dtype=jnp.float32) * 0.02, 'b1': jnp.zeros((E, H), dtype=jnp.float32), 'W2': jax.random.normal(k_w2, (E, H, D), dtype=jnp.float32) * 0.02, 'b2': jnp.zeros((E, D), dtype=jnp.float32)}
        return inp
    _L0_ffn_in = _L0_ffn_setup()
    _L0_c = _w((lambda *s: np.random.randn(*s).astype(np.float32) * 0.05)(16, 128))
    _L0_wmod = _w((lambda *s: np.random.randn(*s).astype(np.float32) * 0.05)(128, 6 * 128) * 128 ** (-0.5))
    _d = {'L0_attn_x': _L0_attn_in['x'], 'L0_attn_wq': _L0_attn_in['wq'], 'L0_attn_wk': _L0_attn_in['wk'], 'L0_attn_wv': _L0_attn_in['wv'], 'L0_attn_wo': _L0_attn_in['wo'], 'L0_attn_wg1': _L0_attn_in['wg1'], 'L0_attn_wg2': _L0_attn_in['wg2'], 'L0_attn_norm_w': _L0_attn_in['norm_w'], 'L0_ffn_Wg': _L0_ffn_in['Wg'], 'L0_ffn_W1': _L0_ffn_in['W1'], 'L0_ffn_b1': _L0_ffn_in['b1'], 'L0_ffn_W2': _L0_ffn_in['W2'], 'L0_ffn_b2': _L0_ffn_in['b2'], 'L0_c': _L0_c, 'L0_wmod': _L0_wmod}
    _x0 = _d['L0_attn_x']
    _d['L0_attn_x'] = jax.random.normal(jax.random.fold_in(jax.random.key(seed), 1), (16, 256, 128), dtype=_x0.dtype)
    del _x0
    return _d

def reference(L0_attn_x, L0_attn_wq, L0_attn_wk, L0_attn_wv, L0_attn_wo, L0_attn_wg1, L0_attn_wg2, L0_attn_norm_w, L0_ffn_Wg, L0_ffn_W1, L0_ffn_b1, L0_ffn_W2, L0_ffn_b2, L0_c, L0_wmod):

    def _L0_attn_ref(x, wq, wk, wv, wo, wg1, wg2, norm_w):
        import jax, jax.numpy as jnp
        import numpy as np
        EMBED = 128
        EXPAND = 128
        B, T = (4, 256)
        PI = 3.141592653589793
        EPS = 1e-05

        def _gla_scan(q, k, v, g):
            Bq, Tq, H, Dk = q.shape
            Dv = v.shape[-1]
            scale = Dk ** (-0.5)

            def step(S, inp):
                qt, kt, vt, gt = inp
                S = S * jnp.exp(gt)[..., None] + kt[..., None] * vt[..., None, :]
                o = jnp.einsum('bhk,bhkv->bhv', qt * scale, S)
                return (S, o)
            S0 = jnp.zeros((Bq, H, Dk, Dv), q.dtype)
            seq = tuple((jnp.moveaxis(a, 1, 0) for a in (q, k, v, g)))
            _, out = jax.lax.scan(step, S0, seq)
            return jnp.moveaxis(out, 0, 1)
        Bx, Tx, E = x.shape
        d = EXPAND
        H = E // d
        q = jax.nn.silu(x @ wq)
        k = jax.nn.sigmoid(x @ wk)
        v = x @ wv
        f = 1.0 - k
        log_f = jnp.log(f)
        q4 = q.reshape(Bx, Tx, H, d)
        k4 = k.reshape(Bx, Tx, H, d)
        v4 = v.reshape(Bx, Tx, H, d)
        f4 = f.reshape(Bx, Tx, H, d)
        g4 = log_f.reshape(Bx, Tx, H, d)
        sign_f = jnp.sign(f4 - 0.5)
        theta = jnp.cumsum(sign_f, axis=1) * PI
        sin, cos = (jnp.sin(theta), jnp.cos(theta))
        qr = jnp.concatenate([q4 * cos, q4 * sin], axis=-1)
        kr = jnp.concatenate([k4 * cos, k4 * sin], axis=-1)
        g = jnp.concatenate([g4, g4], axis=-1)
        out = _gla_scan(qr, kr, v4, g)
        out = out.reshape(Bx, Tx, E)
        gate = jax.nn.sigmoid(x @ wg1 @ wg2)
        out = out * gate
        mu = jnp.mean(out, axis=-1, keepdims=True)
        var = jnp.mean(jnp.square(out - mu), axis=-1, keepdims=True)
        out = (out - mu) * jax.lax.rsqrt(var + EPS) * norm_w
        return out @ wo

    def _L0_ffn_ref(input, Wg, W1, b1, W2, b2):
        import jax, jax.numpy as jnp
        import numpy as np
        E = 8
        D = 128
        H = 256
        TOP_K = 2
        logits = jnp.einsum('bsd,de->bse', input, Wg)
        probs = jax.nn.softmax(logits, axis=-1)
        top_vals, top_idx = jax.lax.top_k(probs, TOP_K)
        top_vals = top_vals / jnp.sum(top_vals, axis=-1, keepdims=True)
        onehot = jax.nn.one_hot(top_idx, E, dtype=input.dtype)
        mask = jnp.sum(onehot, axis=2)
        scores = jnp.sum(onehot * top_vals[..., None], axis=2)
        xm = input[None] * jnp.moveaxis(mask, -1, 0)[..., None]
        h = jnp.einsum('ebsd,edh->ebsh', xm, W1) + b1[:, None, None, :]
        h = jax.nn.relu(h)
        y = jnp.einsum('ebsh,ehd->ebsd', h, W2) + b2[:, None, None, :]
        out = jnp.sum(y * jnp.moveaxis(scores, -1, 0)[..., None], axis=0)
        return out
    x = L0_attn_x
    mod = (_silu(L0_c) @ L0_wmod).reshape(L0_c.shape[0], 6, 1, -1)
    sa, ca, ga, sb, cb, gb = (mod[:, 0], mod[:, 1], mod[:, 2], mod[:, 3], mod[:, 4], mod[:, 5])
    ga = (2 * (ga >= 0) - 1) * jnp.maximum(jnp.abs(ga), 0.25)
    gb = (2 * (gb >= 0) - 1) * jnp.maximum(jnp.abs(gb), 0.25)
    h = _layernorm(x, axis=-1) * (1 + ca) + sa
    x = x + ga * _L0_attn_ref(h, L0_attn_wq, L0_attn_wk, L0_attn_wv, L0_attn_wo, L0_attn_wg1, L0_attn_wg2, L0_attn_norm_w)
    h = _layernorm(x, axis=-1) * (1 + cb) + sb
    x = x + gb * _L0_ffn_ref(h, L0_ffn_Wg, L0_ffn_W1, L0_ffn_b1, L0_ffn_W2, L0_ffn_b2)
    return x

_drawn_inputs = setup_inputs


def setup_inputs(seed=0):
    import zlib

    import numpy as np

    out = dict(_drawn_inputs(seed))
    spreads = {'L0_attn_norm_w': (1.0, 0.6), 'L0_ffn_b1': (0.0, 0.8), 'L0_ffn_b2': (0.0, 0.462)}
    factors = {'L0_attn_wk': 8.0,
     'L0_attn_wg1': 8.0,
     'L0_attn_wg2': 8.0,
     'L0_ffn_Wg': 3.177,
     'L0_ffn_W1': 7.309,
     'L0_ffn_W2': 5.706}
    for name, (base, spread) in spreads.items():
        noise = np.random.default_rng([zlib.crc32(name.encode()), seed]).standard_normal(out[name].shape)
        drawn = base * np.exp(spread * noise) if base else spread * noise
        out[name] = jnp.asarray(drawn.astype(out[name].dtype))
    for name, factor in factors.items():
        out[name] = (out[name] * factor).astype(out[name].dtype)
    return out
```

```python
from contextlib import ExitStack

import concourse.bass as bass
from concourse import mybir

ALU = mybir.AluOpType
ACT = mybir.ActivationFunctionType
AX = mybir.AxisListType
F32 = mybir.dt.float32
F32R = mybir.dt.float32r
I32 = mybir.dt.int32

P = 128
EPS = 1e-5
FLOOR = 0.25
LOWEST = -3.0e38

ATTENTION = {"stats1", "norm1", "proj", "vgate", "diag", "level", "cross", "mix", "norm2", "out", "norm3", "route"}
ORDER = [
    ("stats1", 0), ("up", 0), ("turn", 0), ("norm1", 0), ("up", 1), ("bias", 0), ("down", 0), ("proj", 0),
    ("up", 2), ("vgate", 0), ("down", 1), ("diag", 0), ("level", 1), ("up", 3), ("level", 2), ("down", 2),
    ("level", 3), ("up", 4), ("level", 4), ("down", 3), ("level", 5), ("up", 5), ("level", 6), ("level", 7),
    ("cross", 0), ("down", 4), ("mix", 0), ("up", 6), ("down", 5), ("norm2", 0), ("up", 7), ("out", 0),
    ("down", 6), ("norm3", 0), ("down", 7), ("route", 0), ("final", 0),
]


def adaln_block_kernel(nc, x, wq, wk, wv, wo, wg1, wg2, norm_w, Wg, W1, b1, W2, b2, c, wmod, out):
    B, T, D = x.shape
    E, _, H = W1.shape
    GROUP = 512
    NG = B * T // GROUP
    NB = GROUP // T
    NT = GROUP // P
    TB = T // P
    HH = H // P
    LEVELS = 7
    assert D == P and T == 2 * P and HH == 2 and NG % 2 == 0 and B <= P and E * HH <= P and E == 8
    QSCALE = float(2 * D) ** -0.5

    xg = x.rearrange("b t d -> (b t) d").rearrange("(g c p) d -> g p c d", p=P, c=NT)
    outg = out.rearrange("b t d -> (b t) d").rearrange("(g c p) d -> g p c d", p=P, c=NT)

    with ExitStack() as ctx:
        def sb(name, shape, dt=F32):
            return ctx.enter_context(nc.sbuf_tensor(name, shape, dt))

        def sem(name):
            return ctx.enter_context(nc.semaphore(name))

        def sems(name, n):
            return [sem(f"{name}{i}") for i in range(n)]

        hid_ps = [ctx.enter_context(nc.psum_tensor(f"hid_ps{i}", [P, GROUP], F32)) for i in range(2)]
        y_ps = [ctx.enter_context(nc.psum_tensor(f"y_ps{i}", [P, NT, D], F32)) for i in range(2)]
        pA, pB, pC, pD = [ctx.enter_context(nc.psum_tensor(f"p{n}", [P, GROUP], F32)) for n in "ABCD"]
        LEVEL_BANK = [pB, pC, pD, pA, pB, pC, pD, pA]

        ident = sb("ident", [P, P])
        level_mask = sb("level_mask", [P, 5, GROUP // 2])
        idle = sb("idle", [P, 1])
        ones = sb("ones", [P, GROUP // 2])
        minus_half = sb("minus_half", [P, NT])
        eps4 = sb("eps4", [P, NT])
        first_wins = sb("first_wins", [P, NT * E])
        wq_sb, wk_sb = sb("wq_sb", [D, D]), sb("wk_sb", [D, D])
        wvg_sb = sb("wvg_sb", [D, 2 * D])
        wg1_sb, wg2_sb, wg1T = sb("wg1_sb", [D, D]), sb("wg2_sb", [D, D]), sb("wg1T", [D, D])
        wo_sb, won = sb("wo_sb", [D, D]), sb("won", [D, D])
        nw_sb = sb("nw_sb", [D, 1])
        wr_sb = sb("wr_sb", [D, E])
        b2_sb = sb("b2_sb", [E, D])
        b1_rows, b1T = sb("b1_rows", [E * HH, P]), sb("b1T", [P, E * HH])
        w1_sb = sb("w1_sb", [D, E, H])
        w1_hi, w1_lo = sb("w1_hi", [D, E, H], F32R), sb("w1_lo", [D, E, H], F32R)
        w2_sb = sb("w2_sb", [P, E, HH, D])
        c_sb, c_sig, c_act, cT = sb("c_sb", [B, D]), sb("c_sig", [B, D]), sb("c_act", [B, D]), sb("cT", [D, B])
        wmod_sb = sb("wmod_sb", [D, 6, D])
        modT = sb("modT", [D, 4, B])
        g_raw, g_sign, g_mag, g_rows = (sb(n, [B, 2 * D]) for n in ("g_raw", "g_sign", "g_mag", "g_rows"))
        gates = sb("gates", [P, B, 2 * D])
        x_sb, x2, acc, res = (sb(n, [P, 2, NT, D]) for n in ("x_sb", "x2", "acc", "res"))
        wog = sb("wog", [D, 2, NB, D])
        h2T = sb("h2T", [D, 2, GROUP])
        h2_hi, h2_lo = sb("h2_hi", [D, 2, GROUP], F32R), sb("h2_lo", [D, 2, GROUP], F32R)
        score = sb("score", [P, 2, NT, E])
        stat = sb("stat", [P, 3, NT, 6])
        mean_var = sb("mean_var", [P, 3, NT, 2])
        var_eps, rstd = sb("var_eps", [P, 3, NT]), sb("rstd", [P, 3, NT])
        xn, on, x2n, og = (sb(n, [P, NT, D]) for n in ("xn", "on", "x2n", "og"))
        hT, onT = sb("hT", [D, GROUP]), sb("onT", [D, GROUP])
        q_sig, qraw, f, sgn = (sb(n, [D, GROUP]) for n in ("q_sig", "qraw", "f", "sgn"))
        qk = sb("qk", [D, 2, GROUP])
        decay = [sb(f"decay{m}", [D, GROUP >> m]) for m in range(LEVELS)]
        gate, v = sb("gate", [P, NT, D]), sb("v", [P, NT, D])
        at = sb("at", [P, NT, P])
        ct = sb("ct", [P, NB, P])
        sT = sb("sT", [E, GROUP])
        hid = sb("hid", [P, 2, HH, GROUP])
        eq, cand, pick1, rest, pick2, part = (
            sb(n, [P, NT, E]) for n in ("eq", "cand", "pick1", "rest", "pick2", "part"))
        top1, top2, best, lead, s1, s2 = (sb(n, [P, NT]) for n in ("top1", "top2", "best", "lead", "s1", "s2"))

        x_loaded, cond_loaded, gate_w_loaded, qkv_loaded, out_w_loaded, expert_small_loaded = map(sem, (
            "x_loaded_even", "cond_loaded", "gate_w_loaded", "qkv_loaded", "out_w_loaded", "expert_small_loaded"))
        x_loaded = [x_loaded, sem("x_loaded_odd")]
        w1_loaded, w2_loaded, out_stored = sem("w1_loaded"), sem("w2_loaded"), sems("out_stored", 2)
        setup_pool, setup_act, setup_dve, setup_pe = map(sem, ("setup_pool", "setup_act", "setup_dve", "setup_pe"))
        POOL_SETUP = {name: n + 1 for n, name in enumerate(
            ["memsets", "ident", "mask0", "mask1", "mask2", "mask3", "mask4", "masks"])}
        ACT_SETUP = {name: n + 1 for n, name in enumerate(
            ["cond_sigmoid"] + [f"gates{i}" for i in range(B // 2)] + ["w1_hi"])}
        DVE_SETUP = {name: n + 1 for n, name in enumerate(
            ["cond_act", "cond_turned", "wg1_turned", "b1_turned", "mod", "gate_raw", "gate_parts", "gate_floor", "gate_rows",
             "wg12", "won", "w1_lo"])}
        PE_SETUP = {name: n + 1 for n, name in enumerate(
            ["cond", "wg1", "b1", "mod", "gate_rows", "wg12"] + [f"gates{i}" for i in range(B // 2)])}
        stats_done, aggr_done, eps_added, rstd_ready = (
            sems(n, 3) for n in ("stats_done", "aggr_done", "eps_added", "rstd_ready"))
        (xn_ready, xn_ps, hT_ready, q_ps, k_ps, f_ready, q_sig_ready, q_ready, sgn_ready, a_ready,
         og_ready, on_ready, on_ps, onT_ready, out_ps, x2_ready, x2n_ready, x2n_ps, h2T_ready, h2_hi_ready,
         h2_lo_ready, logit_ps, lead_ready, s12_ready, score_ready, score_ps, sT_ready, bias_ps, acc_ready,
         cross_ps, cross_copied, mix_ps, wog_ready, acc_free, res_ready) = map(sem, (
            "xn_ready", "xn_ps", "hT_ready", "q_ps", "k_ps", "f_ready", "q_sig_ready", "q_ready", "sgn_ready",
            "a_ready", "og_ready", "on_ready", "on_ps", "onT_ready", "out_ps", "x2_ready", "x2n_ready", "x2n_ps",
            "h2T_ready", "h2_hi_ready", "h2_lo_ready", "logit_ps", "lead_ready", "s12_ready", "score_ready",
            "score_ps", "sT_ready", "bias_ps", "acc_ready", "cross_ps", "cross_copied", "mix_ps", "wog_ready",
            "acc_free", "res_ready"))
        vg_ps, vg_copied = sems("vg_ps", 2), sems("vg_copied", 2)
        level_ps, level_copied = sems("level_ps", 8), sems("level_copied", 8)
        carried = dict(enumerate(sems("carried", 8), 1))
        route_step = dict(enumerate(sems("route_step", 12), 1))
        up_ps = [sems(f"up_ps{e}_", HH) for e in range(4)]
        hid_ready = [sems(f"hid_ready{e}_", HH) for e in range(4)]
        y_done, acc_done = sems("y_ps_done", E), sems("acc_done", E)

        def expert_count(e, groups):
            return 2 * groups - (e < 4)

        def wait(eng, semaphore, count):
            if not isinstance(count, int) or count > 0:
                eng.wait_ge(semaphore, count)

        def rounds(eng, one_round):
            one_round(0, 0, True, False)
            with eng.Fori(0, NG // 2 - 1) as j:
                one_round(2 * j + 1, 1, True, True)
                one_round(2 * j + 2, 0, True, True)
            one_round(NG - 1, 1, True, True)
            one_round(NG, 0, False, True)

        def halves(m, first_q, first_k, blocks):
            base = qk[:]
            return bass.AP(tensor=base.tensor, offset=first_q,
                           ap=[list(base.ap[0]), [GROUP + first_k - first_q, 2], [2 * m, blocks], [1, m]])

        block = ctx.enter_context(nc.Block())

        @block.sync
        def _(sp):
            sp.dma_start(c_sb[:], c).then_inc(cond_loaded, 16)
            sp.dma_start(x_sb[:, 0], xg[0]).then_inc(x_loaded[0], 16)
            sp.dma_start(wg1_sb[:], wg1).then_inc(gate_w_loaded, 16)
            sp.dma_start(wg2_sb[:], wg2).then_inc(gate_w_loaded, 16)
            sp.dma_start(wo_sb[:], wo).then_inc(out_w_loaded, 16)
            sp.dma_start(nw_sb[:], norm_w.rearrange("(p a) -> p a", a=1)).then_inc(out_w_loaded, 16)
            sp.dma_start(x_sb[:, 1], xg[1]).then_inc(x_loaded[1], 16)
            sp.dma_start(w2_sb[:], W2.rearrange("e (j p) d -> p e j d", p=P)).then_inc(w2_loaded, 16)

            def one_round(g, par, attention, experts):
                if attention and not (isinstance(g, int) and (g == 0 or g == NG - 1)):
                    sp.wait_ge(x2_ready, g)
                    sp.dma_start(x_sb[:, 1 - par], xg[g + 1]).then_inc(x_loaded[1 - par], 16)
                if experts:
                    sp.wait_ge(res_ready, g)
                    sp.dma_start(outg[g - 1], res[:, 1 - par]).then_inc(out_stored[1 - par], 16)

            rounds(sp, one_round)
            for s in out_stored:
                sp.wait_ge(s, 16 * NG // 2)

        @block.gpsimd
        def _(pool):
            pool.memset(ident[:], 0.0)
            pool.memset(ones[:], 1.0)
            pool.memset(minus_half[:], -0.5)
            pool.memset(eps4[:], EPS).then_inc(acc_free, 2)
            pool.iota(first_wins[:], pattern=[[0, NT], [-1, E]], base=E, channel_multiplier=0,
                      allow_small_or_imprecise_dtypes=True).then_inc(setup_pool, 1)
            pool.wait_ge(setup_pool, POOL_SETUP["memsets"])
            pool.affine_select(out=ident[:], in_=ident[:], compare_op=ALU.not_equal, fill=1.0, base=0,
                               pattern=[[-1, P]], channel_multiplier=1).then_inc(setup_pool, 1)
            for i in range(5):
                m = 1 << i
                blocks = P // (2 * m)
                mask = level_mask[:, i].rearrange("p (c b m) -> p c b m", c=NT, m=m)
                pool.affine_select(out=mask, in_=ones[:].rearrange("p (c b m) -> p c b m", c=NT, m=m),
                                   compare_op=ALU.is_ge, fill=0.0, base=0,
                                   pattern=[[0, NT], [-2 * m, blocks], [0, m]],
                                   channel_multiplier=1).then_inc(setup_pool, 1)
                pool.wait_ge(setup_pool, POOL_SETUP[f"mask{i}"])
                last = pool.affine_select(out=mask, in_=mask, compare_op=ALU.is_ge, fill=0.0, base=m - 1,
                                          pattern=[[0, NT], [2 * m, blocks], [0, m]], channel_multiplier=-1)
            last.then_inc(setup_pool, 1)

            def inverse_deviation(i, now):
                pool.wait_ge(aggr_done[i], now)
                pool.tensor_tensor(var_eps[:, i], mean_var[:, i, :, 1], eps4[:], ALU.add).then_inc(eps_added[i], 1)
                pool.wait_ge(eps_added[i], now)
                pool.tensor_tensor(rstd[:, i], var_eps[:, i], minus_half[:], ALU.pow).then_inc(rstd_ready[i], 1)

            def one_round(g, par, attention, experts):
                now, before, older = g + 1, g, g - 1
                for step, _ in ORDER:
                    if step in ATTENTION and not attention:
                        continue
                    if step == "stats1":
                        inverse_deviation(0, now)
                    elif step == "norm1":
                        wait(pool, out_ps, older)
                        if isinstance(g, int) and g == 0:
                            pool.wait_ge(setup_dve, DVE_SETUP["won"])
                            pool.wait_ge(setup_act, ACT_SETUP[f"gates{B // 2 - 1}"])
                        pool.tensor_tensor(
                            wog[:, par], won[:].unsqueeze(1).to_broadcast([D, NB, D]),
                            gates[:, bass.ds(g * NB, NB), 0:D], ALU.mult).then_inc(wog_ready, 1)
                    elif step == "mix":
                        inverse_deviation(1, now)
                    elif step == "out":
                        inverse_deviation(2, now)
                    elif step == "final" and experts:
                        a, r = acc[:, 1 - par], res[:, 1 - par]
                        pool.wait_ge(acc_done[E - 1], before)
                        gb = gates[:, bass.ds((g - 1) * NB, NB), D:2 * D]
                        if not isinstance(g, int) or g > 2:
                            half = g // 2 if isinstance(g, int) else None
                            pool.wait_ge(out_stored[1 - par], stored_count(g, par))
                        for b in range(NB):
                            last = pool.tensor_tensor(
                                r[:, b * TB:(b + 1) * TB], a[:, b * TB:(b + 1) * TB],
                                gates[:, bass.ds((g - 1) * NB + b, 1), D:2 * D].to_broadcast([P, TB, D]), ALU.mult)
                        last.then_inc(acc_free, 1)
                        pool.wait_ge(acc_free, now + 1)
                        pool.tensor_tensor(r, r, x2[:, 1 - par], ALU.add).then_inc(res_ready, 1)

            def stored_count(g, par):
                if isinstance(g, int):
                    return 16 * ((g - 3) // 2 + 1)
                return 8 * (g - 1) if par == 1 else 8 * (g - 2)

            rounds(pool, one_round)

        @block.scalar
        def _(act):
            act.dma_start(wmod_sb[:], wmod.rearrange("k (j d) -> k j d", d=D)).then_inc(cond_loaded, 16)
            act.dma_start(wq_sb[:], wq).then_inc(qkv_loaded, 16)
            act.dma_start(wk_sb[:], wk).then_inc(qkv_loaded, 16)
            act.dma_start(wvg_sb[:, 0:D], wv).then_inc(qkv_loaded, 16)
            act.dma_start(b1_rows[:], b1.rearrange("e (j p) -> (e j) p", p=P)).then_inc(expert_small_loaded, 16)
            act.dma_start(b2_sb[:], b2).then_inc(expert_small_loaded, 16)
            act.dma_start(wr_sb[:], Wg).then_inc(expert_small_loaded, 16)
            act.dma_start(w1_sb[:], W1.rearrange("e d h -> d e h")).then_inc(w1_loaded, 16)
            act.wait_ge(cond_loaded, 32)
            act.activation(c_sig[:], c_sb[:], ACT.Sigmoid).then_inc(setup_act, 1)
            for i in range(B // 2):
                act.wait_ge(setup_pe, PE_SETUP[f"gates{i}"])
                act.activation(gates[:, 2 * i:2 * i + 2], (hid_ps[i // 2 % 2] if i % 2 == 0 else y_ps[i // 2 % 2])[:],
                               ACT.Copy).then_inc(setup_act, 1)
            act.wait_ge(w1_loaded, 16)
            act.activation(w1_hi[:], w1_sb[:], ACT.Copy).then_inc(setup_act, 1)

            def modulated(out_tile, ps, which, g):
                for b in range(NB):
                    s = slice(b * T, (b + 1) * T)
                    last = act.activation(out_tile[:, s], ps[:, s], ACT.Identity,
                                          scale=modT[:, 2 * which + 1, bass.ds(g * NB + b, 1)],
                                          bias=modT[:, 2 * which, bass.ds(g * NB + b, 1)])
                return last

            def one_round(g, par, attention, experts):
                now, before, older = g + 1, g, g - 1
                for step, i in ORDER:
                    if step in ATTENTION and not attention:
                        continue
                    if step == "norm1":
                        act.wait_ge(xn_ps, now)
                        if isinstance(g, int) and g == 0:
                            act.wait_ge(setup_dve, DVE_SETUP["mod"])
                        wait(act, vg_ps[1], before)
                        modulated(hT, pA, 0, g).then_inc(hT_ready, 1)
                    elif step == "proj":
                        act.wait_ge(k_ps, now)
                        wait(act, cross_ps, before)
                        act.activation(qk[:, 1], pC[:], ACT.Sigmoid)
                        wait(act, carried[1], before)
                        act.activation(f[:], pC[:], ACT.Sigmoid, scale=-1.0).then_inc(f_ready, 1)
                        act.wait_ge(q_ps, now)
                        act.activation(q_sig[:], pB[:], ACT.Sigmoid).then_inc(q_sig_ready, 1)
                    elif step == "vgate":
                        wait(act, mix_ps, before)
                        wait(act, og_ready, before)
                        for h, ps in enumerate((pD, pA)):
                            vg = ps[:].rearrange("p (c d) -> p c d", c=2)
                            act.wait_ge(vg_ps[h], now)
                            act.activation(gate[:, 2 * h:2 * h + 2], vg[:, :, D:2 * D], ACT.Sigmoid)
                            act.activation(v[:, 2 * h:2 * h + 2], vg[:, :, 0:D], ACT.Copy).then_inc(vg_copied[h], 1)
                    elif step == "level" and i == 6:
                        act.wait_ge(level_ps[6], now)
                        act.wait_ge(level_copied[5], now)
                        ps = pD[:, 0:GROUP // 2].rearrange("p (c t) -> p c t", c=NT)
                        act.activation(at[0:32, :, 32:64], ps[0:32, :, 0:32], ACT.Copy)
                        act.activation(at[64:96, :, 96:128], ps[64:96, :, 32:64], ACT.Copy).then_inc(level_copied[6], 1)
                    elif step == "level" and i == 7:
                        act.wait_ge(level_ps[7], now)
                        ps = pA[:, 0:GROUP // 2].rearrange("p (c t) -> p c t", c=NT)
                        act.activation(at[0:64, :, 64:128], ps[0:64], ACT.Copy).then_inc(level_copied[7], 1)
                    elif step == "cross":
                        act.wait_ge(cross_ps, now)
                        act.activation(ct[:], pB[:, 0:NB * P].rearrange("p (b t) -> p b t", b=NB),
                                       ACT.Copy).then_inc(cross_copied, 1)
                    elif step == "norm2":
                        act.wait_ge(on_ps, now)
                        act.activation(onT[:], pD[:], ACT.Copy).then_inc(onT_ready, 1)
                    elif step == "norm3":
                        act.wait_ge(x2n_ps, now)
                        wait(act, up_ps[3][HH - 1], 2 * older)
                        wait(act, h2_lo_ready, older)
                        modulated(h2T[:, par], pB, 1, g).then_inc(h2T_ready, 1)
                        act.wait_ge(h2T_ready, now)
                        act.activation(h2_hi[:, par], h2T[:, par], ACT.Copy).then_inc(h2_hi_ready, 1)
                    elif step == "route":
                        act.wait_ge(lead_ready, now)
                        act.activation(s1[:], lead[:], ACT.Sigmoid)
                        act.activation(s2[:], lead[:], ACT.Sigmoid, scale=-1.0).then_inc(s12_ready, 1)
                    elif step == "turn" and experts:
                        act.wait_ge(score_ps, before)
                        act.activation(sT[:], pD[0:E, :], ACT.Copy).then_inc(sT_ready, 1)
                    elif step == "bias" and experts:
                        act.wait_ge(bias_ps, before)
                        act.wait_ge(acc_free, before)
                        act.activation(acc[:, 1 - par], pA[:].rearrange("p (c d) -> p c d", c=NT),
                                       ACT.Copy).then_inc(acc_ready, 1)
                    elif step == "up" and experts:
                        if i >= 2:
                            act.wait_ge(y_done[i - 2], before)
                        else:
                            wait(act, y_done[i + E - 2], older)
                        for j in range(HH):
                            act.wait_ge(up_ps[i % 4][j], expert_count(i, before))
                            act.activation(hid[:, i % 2, j], hid_ps[j][:], ACT.Relu,
                                           bias=b1T[:, i * HH + j:i * HH + j + 1]).then_inc(hid_ready[i % 4][j], 1)

            act.wait_ge(setup_dve, DVE_SETUP["b1_turned"])
            rounds(act, one_round)

        @block.vector
        def _(dve):
            dve.wait_ge(setup_act, ACT_SETUP["cond_sigmoid"])
            dve.tensor_tensor(c_act[:], c_sb[:], c_sig[:], ALU.mult).then_inc(setup_dve, 1)
            dve.wait_ge(setup_pe, PE_SETUP["cond"])
            dve.tensor_copy(cT[:], pA[:, 0:B]).then_inc(setup_dve, 1)
            dve.wait_ge(setup_pe, PE_SETUP["wg1"])
            dve.tensor_copy(wg1T[:], pD[:, 0:D]).then_inc(setup_dve, 1)
            dve.wait_ge(setup_pe, PE_SETUP["b1"])
            dve.tensor_copy(b1T[:], pD[:, D:D + E * HH]).then_inc(setup_dve, 1)
            dve.wait_ge(setup_pe, PE_SETUP["mod"])
            for w in range(4):
                last = dve.tensor_scalar(modT[:, w], pB[:, w * B:(w + 1) * B], float(w % 2), None, ALU.add)
            last.then_inc(setup_dve, 1)
            dve.wait_ge(setup_pe, PE_SETUP["gate_rows"])
            dve.tensor_copy(g_raw[:], pC[0:B, 0:2 * D]).then_inc(setup_dve, 1)
            dve.wait_ge(setup_dve, DVE_SETUP["gate_raw"])
            dve.tensor_scalar(g_sign[:], g_raw[:], 0.0, 2.0, ALU.is_ge, ALU.mult)
            dve.scalar_tensor_tensor(g_mag[:], g_raw[:], -1.0, g_raw[:], ALU.mult, ALU.max).then_inc(setup_dve, 1)
            dve.wait_ge(setup_dve, DVE_SETUP["gate_parts"])
            dve.tensor_scalar(g_mag[:], g_mag[:], FLOOR, None, ALU.max).then_inc(setup_dve, 1)
            dve.wait_ge(setup_dve, DVE_SETUP["gate_floor"])
            dve.scalar_tensor_tensor(g_rows[:], g_sign[:], 1.0, g_mag[:], ALU.subtract, ALU.mult).then_inc(setup_dve, 1)
            dve.wait_ge(setup_pe, PE_SETUP["wg12"])
            dve.tensor_copy(wvg_sb[:, D:2 * D], pA[:, 0:D]).then_inc(setup_dve, 1)
            dve.wait_ge(out_w_loaded, 32)
            dve.tensor_scalar(won[:], wo_sb[:], nw_sb[:, 0:1], None, ALU.mult).then_inc(setup_dve, 1)

            def statistics(i, src, now):
                for t in range(NT):
                    last = dve.bn_stats(stat[:, i, t], src[:, t])
                last.then_inc(stats_done[i], 1)
                dve.wait_ge(stats_done[i], now)
                dve.memset(idle[:], 0.0)
                for t in range(NT):
                    last = dve.bn_aggr(mean_var[:, i, t], stat[:, i, t])
                last.then_inc(aggr_done[i], 1)

            def normalized(i, out_tile, src, now):
                dve.wait_ge(rstd_ready[i], now)
                for t in range(NT):
                    last = dve.tensor_scalar(out_tile[:, t], src[:, t], mean_var[:, i, t, 0:1],
                                             rstd[:, i, t:t + 1], ALU.subtract, ALU.mult)
                return last

            def compound(m):
                pair = decay[m][:].rearrange("p (b two) -> p b two", two=2)
                return dve.tensor_tensor(decay[m + 1][:], pair[:, :, 0], pair[:, :, 1], ALU.mult)

            def route(g, par, now, older):
                dve.wait_ge(logit_ps, now)
                lead_view = [P, NT, E]
                logits = pC[:, 0:NT * E].rearrange("p (c e) -> p c e", c=NT)
                dve.tensor_reduce(top1[:], logits, AX.X, ALU.max).then_inc(route_step[1], 1)

                def first_of(top, src, picked, s):
                    dve.wait_ge(route_step[s], now)
                    dve.tensor_tensor(eq[:], src, top[:].unsqueeze(2).to_broadcast(lead_view),
                                      ALU.is_equal).then_inc(route_step[s + 1], 1)
                    dve.wait_ge(route_step[s + 1], now)
                    dve.tensor_tensor(cand[:], eq[:], first_wins[:].rearrange("p (c e) -> p c e", c=NT),
                                      ALU.mult).then_inc(route_step[s + 2], 1)
                    dve.wait_ge(route_step[s + 2], now)
                    dve.tensor_reduce(best[:], cand[:], AX.X, ALU.max).then_inc(route_step[s + 3], 1)
                    dve.wait_ge(route_step[s + 3], now)
                    dve.tensor_tensor(picked[:], cand[:], best[:].unsqueeze(2).to_broadcast(lead_view),
                                      ALU.is_equal).then_inc(route_step[s + 4], 1)

                first_of(top1, logits, pick1, 1)
                dve.wait_ge(route_step[5], now)
                dve.scalar_tensor_tensor(rest[:], pick1[:], LOWEST, logits, ALU.mult, ALU.add).then_inc(route_step[6], 1)
                dve.wait_ge(route_step[6], now)
                dve.tensor_reduce(top2[:], rest[:], AX.X, ALU.max).then_inc(route_step[7], 1)
                dve.wait_ge(route_step[7], now)
                dve.tensor_tensor(lead[:], top1[:], top2[:], ALU.subtract).then_inc(lead_ready, 1)
                first_of(top2, rest[:], pick2, 7)
                dve.wait_ge(s12_ready, now)
                dve.tensor_tensor(part[:], pick1[:], s1[:].unsqueeze(2).to_broadcast(lead_view), ALU.mult)
                dve.wait_ge(route_step[11], now)
                dve.tensor_tensor(pick2[:], pick2[:], s2[:].unsqueeze(2).to_broadcast(lead_view),
                                  ALU.mult).then_inc(route_step[12], 1)
                dve.wait_ge(route_step[12], now)
                wait(dve, acc_done[E - 1], older)
                wait(dve, score_ps, older)
                dve.tensor_tensor(score[:, par], part[:], pick2[:], ALU.add).then_inc(score_ready, 1)

            def x_count(g, par):
                if isinstance(g, int):
                    return 16 * (g // 2 + 1)
                return 8 * (g + 1) if par == 1 else 8 * (g + 2)

            def one_round(g, par, attention, experts):
                now, before, older = g + 1, g, g - 1
                first = isinstance(g, int) and g == 0
                for step, i in ORDER:
                    if step in ATTENTION and not attention:
                        continue
                    if step == "stats1":
                        dve.wait_ge(x_loaded[par], x_count(g, par))
                        statistics(0, x_sb[:, par], now)
                    elif step == "norm1":
                        normalized(0, xn, x_sb[:, par], now).then_inc(xn_ready, 1)
                    elif step == "proj":
                        dve.wait_ge(q_sig_ready, now)
                        wait(dve, level_ps[0], before)
                        dve.tensor_tensor(qraw[:], pB[:], q_sig[:], ALU.mult).then_inc(q_ready, 1)
                        dve.wait_ge(f_ready, now)
                        dve.tensor_scalar(sgn[:], f[:], 0.5, 2.0, ALU.is_equal, ALU.mult).then_inc(sgn_ready, 1)
                        dve.wait_ge(sgn_ready, now)
                        dve.scalar_tensor_tensor(decay[0][:], sgn[:], 1.0, f[:], ALU.subtract, ALU.mult).then_inc(a_ready, 1)
                        dve.wait_ge(q_ready, now)
                        dve.wait_ge(a_ready, now)
                        wait(dve, cross_ps, before)
                        compound(0)
                        dve.tensor_tensor(qk[:, 0], qraw[:], decay[0][:], ALU.mult).then_inc(carried[1], 1)
                    elif step == "diag":
                        if first:
                            dve.wait_ge(setup_pool, POOL_SETUP["ident"])
                            dve.wait_ge(setup_pool, POOL_SETUP["masks"])
                        dve.wait_ge(level_ps[0], now)
                        wait(dve, mix_ps, before)
                        dve.tensor_tensor(at[:], pB[:].rearrange("p (c t) -> p c t", c=NT),
                                          ident[:].unsqueeze(1).to_broadcast([P, NT, P]), ALU.mult).then_inc(level_copied[0], 1)
                    elif step == "level":
                        m = 1 << (i - 1)
                        dve.wait_ge(level_ps[i], now)
                        dve.wait_ge(carried[i], now)
                        if i < LEVELS:
                            if i <= 5:
                                dve.wait_ge(level_copied[i - 1], now)
                            if i < LEVELS - 1:
                                compound(i)
                            blocks = GROUP // (2 * m)
                            part_view = halves(m, m, 0, blocks)
                            over = decay[i - 1][:].rearrange("p (b two) -> p two b", two=2)
                            dve.tensor_tensor(part_view, part_view, over.unsqueeze(3).to_broadcast([D, 2, blocks, m]),
                                              ALU.mult).then_inc(carried[i + 1], 1)
                        else:
                            over = decay[i - 1][:].rearrange("p (b four) -> p b four", four=4)
                            q2 = qk[:, 0].rearrange("p (b c m) -> p b c m", b=NB, c=4)[:, :, 3]
                            k1 = qk[:, 1].rearrange("p (b c m) -> p b c m", b=NB, c=4)[:, :, 0]
                            dve.tensor_tensor(q2, q2, over[:, :, 2:3].to_broadcast([D, NB, m]), ALU.mult)
                            dve.tensor_tensor(k1, k1, over[:, :, 1:2].to_broadcast([D, NB, m]),
                                              ALU.mult).then_inc(carried[8], 1)
                        if i <= 5:
                            blocks = GROUP // (2 * m)
                            dst = at[:].rearrange("p c t -> p (c t)").rearrange("p (b two m) -> p b two m", two=2, m=m)[:, :, 1]
                            src = LEVEL_BANK[i][:, 0:GROUP // 2].rearrange("p (b m) -> p b m", m=m)
                            msk = level_mask[:, i - 1].bitcast(I32).rearrange("p (b m) -> p b m", m=m)
                            dve.copy_predicated(dst, msk, src).then_inc(level_copied[i], 1)
                    elif step == "mix":
                        dve.wait_ge(mix_ps, now)
                        dve.scalar_tensor_tensor(og[:], pC[:].rearrange("p (c d) -> p c d", c=NT), QSCALE, gate[:],
                                                 ALU.mult, ALU.mult).then_inc(og_ready, 1)
                        dve.wait_ge(og_ready, now)
                        statistics(1, og, now)
                    elif step == "norm2":
                        normalized(1, on, og, now).then_inc(on_ready, 1)
                    elif step == "out":
                        dve.wait_ge(out_ps, now)
                        wait(dve, res_ready, older)
                        dve.tensor_tensor(x2[:, par], pA[:].rearrange("p (c d) -> p c d", c=NT), x_sb[:, par],
                                          ALU.add).then_inc(x2_ready, 1)
                        dve.wait_ge(x2_ready, now)
                        statistics(2, x2[:, par], now)
                    elif step == "norm3":
                        normalized(2, x2n, x2[:, par], now).then_inc(x2n_ready, 1)
                        dve.wait_ge(h2_hi_ready, now)
                        dve.tensor_tensor(h2_lo[:, par], h2T[:, par], h2_hi[:, par].bitcast(F32),
                                          ALU.subtract).then_inc(h2_lo_ready, 1)
                    elif step == "route":
                        route(g, par, now, older)
                    elif step == "down" and experts:
                        dve.wait_ge(y_done[i], before)
                        dve.wait_ge(acc_ready if i == 0 else acc_done[i - 1], before)
                        if i == 0:
                            dve.wait_ge(score_ready, before)
                        for t in range(NT):
                            a = acc[:, 1 - par, t]
                            last = dve.scalar_tensor_tensor(a, y_ps[i % 2][:, t], score[:, 1 - par, t, i:i + 1], a,
                                                            ALU.mult, ALU.add)
                        last.then_inc(acc_done[i], 1)
                if first:
                    dve.wait_ge(setup_act, ACT_SETUP["w1_hi"])
                    dve.tensor_tensor(w1_lo[:], w1_sb[:], w1_hi[:].bitcast(F32), ALU.subtract).then_inc(setup_dve, 1)

            rounds(dve, one_round)

        @block.tensor
        def _(pe):
            def mm(o, lhsT, rhs, start=True, stop=True):
                return pe.matmul(o, lhsT, rhs, start=start, stop=stop)

            pe.wait_ge(setup_pool, POOL_SETUP["ident"])
            pe.wait_ge(setup_dve, DVE_SETUP["cond_act"])
            pe.transpose(pA[:, 0:B], c_act[:], ident[0:B, 0:B]).then_inc(setup_pe, 1)
            pe.wait_ge(gate_w_loaded, 32)
            pe.transpose(pD[:, 0:D], wg1_sb[:], ident[:]).then_inc(setup_pe, 1)
            pe.wait_ge(expert_small_loaded, 48)
            pe.wait_ge(setup_dve, DVE_SETUP["wg1_turned"])
            pe.transpose(pD[:, D:D + E * HH], b1_rows[:], ident[0:E * HH, 0:E * HH]).then_inc(setup_pe, 1)
            pe.wait_ge(setup_dve, DVE_SETUP["cond_turned"])
            for w, j in enumerate((0, 1, 3, 4)):
                last = mm(pB[:, w * B:(w + 1) * B], wmod_sb[:, j], cT[:])
            last.then_inc(setup_pe, 1)
            mm(pC[0:B, 0:D], cT[:], wmod_sb[:, 2])
            mm(pC[0:B, D:2 * D], cT[:], wmod_sb[:, 5]).then_inc(setup_pe, 1)
            mm(pA[:, 0:D], wg1T[:], wg2_sb[:]).then_inc(setup_pe, 1)
            pe.wait_ge(setup_dve, DVE_SETUP["gate_rows"])
            for i in range(B // 2):
                ps = (hid_ps[i // 2 % 2][:] if i % 2 == 0 else y_ps[i // 2 % 2][:].rearrange("p c d -> p (c d)"))
                if i >= 4:
                    pe.wait_ge(setup_act, ACT_SETUP[f"gates{i - 4}"])
                for b in range(2):
                    pick = ident[0:B, 2 * i + b:2 * i + b + 1].to_broadcast([B, P])
                    last = mm(ps[:, b * 2 * D:(b + 1) * 2 * D], pick, g_rows[:])
                last.then_inc(setup_pe, 1)

            def turn(ps, src):
                for t in range(NT):
                    last = pe.transpose(ps[:, t * P:(t + 1) * P], src[:, t], ident[:])
                return last

            def one_round(g, par, attention, experts):
                now, before, older = g + 1, g, g - 1
                first = isinstance(g, int) and g == 0
                for step, i in ORDER:
                    if step in ATTENTION and not attention:
                        continue
                    if step == "norm1":
                        pe.wait_ge(xn_ready, now)
                        if first:
                            pe.wait_ge(setup_dve, DVE_SETUP["wg12"])
                        wait(pe, x2_ready, before)
                        turn(pA, xn).then_inc(xn_ps, 1)
                    elif step == "proj":
                        pe.wait_ge(hT_ready, now)
                        if first:
                            pe.wait_ge(qkv_loaded, 48)
                            pe.wait_ge(setup_dve, DVE_SETUP["mod"])
                            pe.wait_ge(setup_dve, DVE_SETUP["gate_raw"])
                        wait(pe, h2T_ready, before)
                        mm(pB[:], wq_sb[:], hT[:]).then_inc(q_ps, 1)
                        wait(pe, lead_ready, before)
                        mm(pC[:], wk_sb[:], hT[:]).then_inc(k_ps, 1)
                    elif step == "vgate":
                        if first:
                            pe.wait_ge(setup_dve, DVE_SETUP["b1_turned"])
                        for h, ps in enumerate((pD, pA)):
                            if experts:
                                pe.wait_ge(sT_ready if h == 0 else acc_ready, before)
                            for t in range(2):
                                tok = slice((2 * h + t) * P, (2 * h + t + 1) * P)
                                last = mm(ps[:, t * 2 * D:(t + 1) * 2 * D], hT[:, tok], wvg_sb[:])
                            last.then_inc(vg_ps[h], 1)
                    elif step == "diag":
                        pe.wait_ge(q_ready, now)
                        pe.wait_ge(f_ready, now)
                        for t in range(NT):
                            tok = slice(t * P, (t + 1) * P)
                            last = mm(pB[:, tok], qk[:, 1, tok], qraw[:, tok])
                        last.then_inc(level_ps[0], 1)
                    elif step == "level":
                        m = 1 << (i - 1)
                        pe.wait_ge(carried[i], now)
                        if i == 1:
                            pe.wait_ge(f_ready, now)
                        elif i in (2, 3):
                            pe.wait_ge(vg_copied[i - 2], now)
                        else:
                            pe.wait_ge(level_copied[i - 4], now)
                        for t in range(NT):
                            tok = slice(t * P, (t + 1) * P)
                            q_second = qk[:, 0, tok].rearrange("p (b two m) -> p b two m", two=2, m=m)[:, :, 1]
                            last = mm(LEVEL_BANK[i][:, t * P // 2:(t + 1) * P // 2].rearrange("p (b m) -> p b m", m=m),
                                      qk[:, 1, tok], q_second)
                        last.then_inc(level_ps[i], 1)
                    elif step == "cross":
                        pe.wait_ge(carried[8], now)
                        pe.wait_ge(level_copied[4], now)
                        for b in range(NB):
                            s, t = slice(2 * b * P, (2 * b + 1) * P), slice((2 * b + 1) * P, (2 * b + 2) * P)
                            last = mm(pB[:, b * P:(b + 1) * P], qk[:, 1, s], qk[:, 0, t])
                        last.then_inc(cross_ps, 1)
                    elif step == "mix":
                        pe.wait_ge(vg_copied[1], now)
                        pe.wait_ge(level_copied[5], now)
                        pe.wait_ge(cross_copied, now)
                        for t in range(NT):
                            o = pC[:, t * D:(t + 1) * D]
                            later = t % TB == 1
                            last = mm(o, at[:, t], v[:, t], stop=not later)
                            if later:
                                last = mm(o, ct[:, t // TB], v[:, t - 1], start=False)
                        last.then_inc(mix_ps, 1)
                    elif step == "norm2":
                        pe.wait_ge(on_ready, now)
                        pe.wait_ge(level_copied[6], now)
                        turn(pD, on).then_inc(on_ps, 1)
                    elif step == "out":
                        pe.wait_ge(onT_ready, now)
                        pe.wait_ge(wog_ready, now)
                        pe.wait_ge(level_copied[7], now)
                        for t in range(NT):
                            last = mm(pA[:, t * D:(t + 1) * D], onT[:, t * P:(t + 1) * P], wog[:, par, t // TB])
                        last.then_inc(out_ps, 1)
                    elif step == "norm3":
                        pe.wait_ge(x2n_ready, now)
                        turn(pB, x2n).then_inc(x2n_ps, 1)
                    elif step == "route":
                        pe.wait_ge(h2T_ready, now)
                        pe.wait_ge(og_ready, now)
                        for t in range(NT):
                            last = mm(pC[:, t * E:(t + 1) * E], h2T[:, par, t * P:(t + 1) * P], wr_sb[:])
                        last.then_inc(logit_ps, 1)
                    elif step == "turn" and experts:
                        pe.wait_ge(score_ready, before)
                        pe.wait_ge(onT_ready, before)
                        for t in range(NT):
                            last = pe.transpose(pD[0:E, t * P:(t + 1) * P], score[:, 1 - par, t], ident[:])
                        last.then_inc(score_ps, 1)
                    elif step == "bias" and experts:
                        pe.wait_ge(sT_ready, before)
                        pe.wait_ge(hT_ready, now) if attention else pe.wait_ge(x2_ready, before)
                        for t in range(NT):
                            last = mm(pA[:, t * D:(t + 1) * D], sT[:, t * P:(t + 1) * P], b2_sb[:])
                        last.then_inc(bias_ps, 1)
                    elif step == "up" and experts:
                        if i == 0:
                            pe.wait_ge(h2_lo_ready, before)
                            if isinstance(g, int) and g == 1 or not isinstance(g, int):
                                pe.wait_ge(setup_dve, DVE_SETUP["w1_lo"])
                        x_hi, x_lo = h2_hi[:, 1 - par], h2_lo[:, 1 - par]
                        for j in range(HH):
                            if i >= 1:
                                pe.wait_ge(hid_ready[(i - 1) % 4][j], expert_count(i - 1, before))
                            else:
                                wait(pe, hid_ready[3][j], 2 * older)
                            w = slice(j * P, (j + 1) * P)
                            mm(hid_ps[j][:], w1_hi[:, i, w], x_hi, stop=False)
                            mm(hid_ps[j][:], w1_hi[:, i, w], x_lo, start=False, stop=False)
                            mm(hid_ps[j][:], w1_lo[:, i, w], x_hi, start=False).then_inc(up_ps[i % 4][j], 1)
                    elif step == "down" and experts:
                        if i == 0:
                            pe.wait_ge(w2_loaded, 16)
                        pe.wait_ge(hid_ready[i % 4][HH - 1], expert_count(i, before))
                        if i >= 2:
                            pe.wait_ge(acc_done[i - 2], before)
                        else:
                            wait(pe, acc_done[i + E - 2], older)
                        for t in range(NT):
                            for j in range(HH):
                                last = mm(y_ps[i % 2][:, t], hid[:, i % 2, j, t * P:(t + 1) * P], w2_sb[:, i, j],
                                          start=j == 0, stop=j == HH - 1)
                        last.then_inc(y_done[i], 1)

            pe.wait_ge(setup_act, ACT_SETUP[f"gates{B // 2 - 1}"])
            rounds(pe, one_round)


_INS = ["L0_attn_x", "L0_attn_wq", "L0_attn_wk", "L0_attn_wv", "L0_attn_wo", "L0_attn_wg1", "L0_attn_wg2",
        "L0_attn_norm_w", "L0_ffn_Wg", "L0_ffn_W1", "L0_ffn_b1", "L0_ffn_W2", "L0_ffn_b2", "L0_c", "L0_wmod"]


def kernel(**inputs):
    import numpy as _np
    import concourse.bacc as _bacc
    from concourse import mybir as _mybir
    from concourse.bass_utils import run_bass_kernel_spmd as _run

    nc = _bacc.Bacc("TRN2", target_bir_lowering=False, num_devices=1)
    arrays, args = {}, []
    for name in _INS:
        a = _np.ascontiguousarray(inputs[name])
        arrays[f"in_{name}_dram"] = a
        args.append(nc.dram_tensor(f"in_{name}_dram", a.shape, _mybir.dt.from_np(a.dtype), kind="ExternalInput").ap())
    shape = tuple(inputs["L0_attn_x"].shape)
    out = nc.dram_tensor("out_0_dram", shape, _mybir.dt.float32, kind="ExternalOutput").ap()
    adaln_block_kernel(nc, *args, out)
    r = _run(nc, [arrays], core_ids=[0])
    return r.results[0]["out_0_dram"]
```

```python
from contextlib import ExitStack

import concourse.bass as bass
from concourse import mybir

ALU = mybir.AluOpType
ACT = mybir.ActivationFunctionType
AX = mybir.AxisListType
F32 = mybir.dt.float32
F32R = mybir.dt.float32r
I32 = mybir.dt.int32

P = 128
EPS = 1e-5
FLOOR = 0.25
LOWEST = -3.0e38

FRONT = {"stats1", "norm1", "proj", "vgate"}
EXPERTS = {"up", "turn", "bias", "down", "final"}
ORDER = [
    ("turn", 0), ("up", 0), ("bias", 0), ("diag", 0), ("up", 1), ("level", 1), ("down", 0), ("level", 2),
    ("level", 3), ("up", 2), ("level", 4), ("stats1", 0), ("level", 5), ("down", 1), ("level", 6),
    ("level", 7), ("up", 3), ("cross", 0), ("norm1", 0), ("down", 2), ("mix", 0), ("up", 4), ("down", 3),
    ("up", 5), ("norm2", 0), ("down", 4), ("out", 0), ("up", 6), ("down", 5), ("up", 7), ("norm3", 0),
    ("down", 6), ("proj", 0), ("route", 0), ("vgate", 0), ("down", 7), ("final", 0),
]


def adaln_block_kernel(nc, x, wq, wk, wv, wo, wg1, wg2, norm_w, Wg, W1, b1, W2, b2, c, wmod, out):
    B, T, D = x.shape
    E, _, H = W1.shape
    GROUP = 512
    NG = B * T // GROUP
    NB = GROUP // T
    NT = GROUP // P
    TB = T // P
    HH = H // P
    LEVELS = 7
    assert D == P and T == 2 * P and HH == 2 and NG % 2 == 0 and B <= P and E * HH <= P and E == 8
    QSCALE = float(2 * D) ** -0.5

    xg = x.rearrange("b t d -> (b t) d").rearrange("(g c p) d -> g p c d", p=P, c=NT)
    outg = out.rearrange("b t d -> (b t) d").rearrange("(g c p) d -> g p c d", p=P, c=NT)

    with ExitStack() as ctx:
        def sb(name, shape, dt=F32):
            return ctx.enter_context(nc.sbuf_tensor(name, shape, dt))

        def sem(name):
            return ctx.enter_context(nc.semaphore(name))

        def sems(name, n):
            return [sem(f"{name}{i}") for i in range(n)]

        hid_ps = [ctx.enter_context(nc.psum_tensor(f"hid_ps{i}", [P, GROUP], F32)) for i in range(2)]
        y_ps = [ctx.enter_context(nc.psum_tensor(f"y_ps{i}", [P, NT, D], F32)) for i in range(2)]
        pA, pB, pC, pD = [ctx.enter_context(nc.psum_tensor(f"p{n}", [P, GROUP], F32)) for n in "ABCD"]
        LEVEL_BANK = [pB, pC, pD, pA, pB, pC, pD, pA]

        ident = sb("ident", [P, P])
        level_mask = sb("level_mask", [P, 5, GROUP // 2])
        idle = sb("idle", [P, 1])
        ones = sb("ones", [P, GROUP // 2])
        minus_half = sb("minus_half", [P, NT])
        eps4 = sb("eps4", [P, NT])
        first_wins = sb("first_wins", [P, NT * E])
        wq_sb, wk_sb = sb("wq_sb", [D, D]), sb("wk_sb", [D, D])
        wvg_sb = sb("wvg_sb", [D, 2 * D])
        wg1_sb, wg2_sb, wg1T = sb("wg1_sb", [D, D]), sb("wg2_sb", [D, D]), sb("wg1T", [D, D])
        wo_sb, won = sb("wo_sb", [D, D]), sb("won", [D, D])
        nw_sb = sb("nw_sb", [D, 1])
        wr_sb = sb("wr_sb", [D, E])
        b2_sb = sb("b2_sb", [E, D])
        b1_rows, b1T = sb("b1_rows", [E * HH, P]), sb("b1T", [P, E * HH])
        w1_sb = sb("w1_sb", [D, E, H])
        w1_hi, w1_lo = sb("w1_hi", [D, E, H], F32R), sb("w1_lo", [D, E, H], F32R)
        w2_sb = sb("w2_sb", [P, E, HH, D])
        c_sb, c_sig, c_act, cT = sb("c_sb", [B, D]), sb("c_sig", [B, D]), sb("c_act", [B, D]), sb("cT", [D, B])
        wmod_sb = sb("wmod_sb", [D, 6, D])
        modT = sb("modT", [D, 4, B])
        g_raw, g_sign, g_mag, g_rows = (sb(n, [B, 2 * D]) for n in ("g_raw", "g_sign", "g_mag", "g_rows"))
        gates = sb("gates", [P, B, 2 * D])
        x_sb, x2, acc, res = (sb(n, [P, 2, NT, D]) for n in ("x_sb", "x2", "acc", "res"))
        wog = sb("wog", [D, 2, NB, D])
        h2T = sb("h2T", [D, 2, GROUP])
        h2_hi, h2_lo = sb("h2_hi", [D, 2, GROUP], F32R), sb("h2_lo", [D, 2, GROUP], F32R)
        score = sb("score", [P, 2, NT, E])
        stat = sb("stat", [P, 3, NT, 6])
        mean_var = sb("mean_var", [P, 3, NT, 2])
        var_eps, rstd = sb("var_eps", [P, 3, NT]), sb("rstd", [P, 3, NT])
        xn, on, x2n, og = (sb(n, [P, NT, D]) for n in ("xn", "on", "x2n", "og"))
        hT, onT = sb("hT", [D, GROUP]), sb("onT", [D, GROUP])
        q_sig, qraw, f, sgn = (sb(n, [D, GROUP]) for n in ("q_sig", "qraw", "f", "sgn"))
        qk = sb("qk", [D, 2, GROUP])
        decay = [sb(f"decay{m}", [D, GROUP >> m]) for m in range(LEVELS)]
        gate, v = sb("gate", [P, NT, D]), sb("v", [P, NT, D])
        at = sb("at", [P, NT, P])
        ct = sb("ct", [P, NB, P])
        sT = sb("sT", [E, GROUP])
        hid = sb("hid", [P, 2, HH, GROUP])
        eq, cand, pick1, rest, pick2, part = (
            sb(n, [P, NT, E]) for n in ("eq", "cand", "pick1", "rest", "pick2", "part"))
        top1, top2, best, lead, s1, s2 = (sb(n, [P, NT]) for n in ("top1", "top2", "best", "lead", "s1", "s2"))

        x_loaded, cond_loaded, gate_w_loaded, qkv_loaded, out_w_loaded, expert_small_loaded = map(sem, (
            "x_loaded_even", "cond_loaded", "gate_w_loaded", "qkv_loaded", "out_w_loaded", "expert_small_loaded"))
        x_loaded = [x_loaded, sem("x_loaded_odd")]
        w1_loaded, w2_loaded, out_stored = sem("w1_loaded"), sem("w2_loaded"), sems("out_stored", 2)
        setup_pool, setup_act, setup_dve, setup_pe = map(sem, ("setup_pool", "setup_act", "setup_dve", "setup_pe"))
        POOL_SETUP = {name: n + 1 for n, name in enumerate(
            ["memsets", "ident", "mask0", "mask1", "mask2", "mask3", "mask4", "masks"])}
        ACT_SETUP = {name: n + 1 for n, name in enumerate(
            ["cond_sigmoid"] + [f"gates{i}" for i in range(B // 2)] + ["w1_hi"])}
        DVE_SETUP = {name: n + 1 for n, name in enumerate(
            ["cond_act", "cond_turned", "wg1_turned", "b1_turned", "mod", "gate_raw", "gate_parts", "gate_floor", "gate_rows",
             "wg12", "won", "w1_lo"])}
        PE_SETUP = {name: n + 1 for n, name in enumerate(
            ["cond", "wg1", "b1", "mod", "gate_rows", "wg12"] + [f"gates{i}" for i in range(B // 2)])}
        stats_done, aggr_done, eps_added, rstd_ready = (
            sems(n, 3) for n in ("stats_done", "aggr_done", "eps_added", "rstd_ready"))
        (xn_ready, xn_ps, hT_ready, q_ps, k_ps, f_ready, q_sig_ready, q_ready, sgn_ready, a_ready,
         og_ready, on_ready, on_ps, onT_ready, out_ps, x2_ready, x2n_ready, x2n_ps, h2T_ready, h2_hi_ready,
         h2_lo_ready, logit_ps, lead_ready, s12_ready, score_ready, score_ps, sT_ready, bias_ps, acc_ready,
         cross_ps, cross_copied, mix_ps, wog_ready, acc_free, res_ready) = map(sem, (
            "xn_ready", "xn_ps", "hT_ready", "q_ps", "k_ps", "f_ready", "q_sig_ready", "q_ready", "sgn_ready",
            "a_ready", "og_ready", "on_ready", "on_ps", "onT_ready", "out_ps", "x2_ready", "x2n_ready", "x2n_ps",
            "h2T_ready", "h2_hi_ready", "h2_lo_ready", "logit_ps", "lead_ready", "s12_ready", "score_ready",
            "score_ps", "sT_ready", "bias_ps", "acc_ready", "cross_ps", "cross_copied", "mix_ps", "wog_ready",
            "acc_free", "res_ready"))
        vg_ps, vg_copied = sems("vg_ps", 2), sems("vg_copied", 2)
        level_ps, level_copied = sems("level_ps", 8), sems("level_copied", 8)
        carried = dict(enumerate(sems("carried", 8), 1))
        route_step = dict(enumerate(sems("route_step", 12), 1))
        up_ps = [sems(f"up_ps{e}_", HH) for e in range(4)]
        hid_ready = [sems(f"hid_ready{e}_", HH) for e in range(4)]
        y_done, acc_done = sems("y_ps_done", E), sems("acc_done", E)

        def done(group):
            return group + 2

        def expert_count(e, groups):
            return 2 * groups - (e < 4)

        def wait(eng, semaphore, count):
            if not isinstance(count, int) or count > 1:
                eng.wait_ge(semaphore, count)

        def start_ahead(eng, once, twice=()):
            for s in once:
                eng.sem_inc(s, 1)
            for s in twice:
                eng.sem_inc(s, 2)

        def rounds(eng, one_round):
            one_round(-1, 1, front=True, attention=False, experts=False)
            one_round(0, 0, front=True, attention=True, experts=False)
            with eng.Fori(0, NG // 2 - 1) as j:
                one_round(2 * j + 1, 1, front=True, attention=True, experts=True)
                one_round(2 * j + 2, 0, front=True, attention=True, experts=True)
            one_round(NG - 1, 1, front=False, attention=True, experts=True)
            one_round(NG, 0, front=False, attention=False, experts=True)

        def steps(front, attention, experts):
            return [(s, i) for s, i in ORDER
                    if (front if s in FRONT else experts if s in EXPERTS else attention)]

        def halves(m, first_q, first_k, blocks):
            base = qk[:]
            return bass.AP(tensor=base.tensor, offset=first_q,
                           ap=[list(base.ap[0]), [GROUP + first_k - first_q, 2], [2 * m, blocks], [1, m]])

        block = ctx.enter_context(nc.Block())

        @block.sync
        def _(sp):
            sp.dma_start(c_sb[:], c).then_inc(cond_loaded, 16)
            sp.dma_start(x_sb[:, 0], xg[0]).then_inc(x_loaded[0], 16)
            sp.dma_start(wg1_sb[:], wg1).then_inc(gate_w_loaded, 16)
            sp.dma_start(wg2_sb[:], wg2).then_inc(gate_w_loaded, 16)
            sp.dma_start(wo_sb[:], wo).then_inc(out_w_loaded, 16)
            sp.dma_start(nw_sb[:], norm_w.rearrange("(p a) -> p a", a=1)).then_inc(out_w_loaded, 16)
            sp.dma_start(x_sb[:, 1], xg[1]).then_inc(x_loaded[1], 16)
            sp.dma_start(w2_sb[:], W2.rearrange("e (j p) d -> p e j d", p=P)).then_inc(w2_loaded, 16)

            def one_round(g, par, front, attention, experts):
                if front and not (isinstance(g, int) and g < 1):
                    sp.wait_ge(x2_ready, done(g - 1))
                    sp.dma_start(x_sb[:, 1 - par], xg[g + 1]).then_inc(x_loaded[1 - par], 16)
                if experts:
                    sp.wait_ge(res_ready, done(g - 1))
                    sp.dma_start(outg[g - 1], res[:, 1 - par]).then_inc(out_stored[1 - par], 16)

            rounds(sp, one_round)
            for s in out_stored:
                sp.wait_ge(s, 16 * (NG // 2 + 1))

        @block.gpsimd
        def _(pool):
            pool.memset(ident[:], 0.0)
            pool.memset(ones[:], 1.0)
            pool.memset(minus_half[:], -0.5)
            pool.memset(eps4[:], EPS).then_inc(acc_free, 2)
            pool.iota(first_wins[:], pattern=[[0, NT], [-1, E]], base=E, channel_multiplier=0,
                      allow_small_or_imprecise_dtypes=True).then_inc(setup_pool, 1)
            pool.wait_ge(setup_pool, POOL_SETUP["memsets"])
            pool.affine_select(out=ident[:], in_=ident[:], compare_op=ALU.not_equal, fill=1.0, base=0,
                               pattern=[[-1, P]], channel_multiplier=1).then_inc(setup_pool, 1)
            for i in range(5):
                m = 1 << i
                blocks = P // (2 * m)
                mask = level_mask[:, i].rearrange("p (c b m) -> p c b m", c=NT, m=m)
                pool.affine_select(out=mask, in_=ones[:].rearrange("p (c b m) -> p c b m", c=NT, m=m),
                                   compare_op=ALU.is_ge, fill=0.0, base=0,
                                   pattern=[[0, NT], [-2 * m, blocks], [0, m]],
                                   channel_multiplier=1).then_inc(setup_pool, 1)
                pool.wait_ge(setup_pool, POOL_SETUP[f"mask{i}"])
                last = pool.affine_select(out=mask, in_=mask, compare_op=ALU.is_ge, fill=0.0, base=m - 1,
                                          pattern=[[0, NT], [2 * m, blocks], [0, m]], channel_multiplier=-1)
            last.then_inc(setup_pool, 1)

            def inverse_deviation(i, now):
                pool.wait_ge(aggr_done[i], now)
                pool.tensor_tensor(var_eps[:, i], mean_var[:, i, :, 1], eps4[:], ALU.add).then_inc(eps_added[i], 1)
                pool.wait_ge(eps_added[i], now)
                pool.tensor_tensor(rstd[:, i], var_eps[:, i], minus_half[:], ALU.pow).then_inc(rstd_ready[i], 1)

            def one_round(g, par, front, attention, experts):
                ahead, now, before, older = done(g + 1), done(g), done(g - 1), done(g - 2)
                for step, _ in steps(front, attention, experts):
                    if step == "stats1":
                        inverse_deviation(0, ahead)
                    elif step == "diag":
                        wait(pool, out_ps, older)
                        if isinstance(g, int) and g == 0:
                            pool.wait_ge(setup_dve, DVE_SETUP["won"])
                            pool.wait_ge(setup_act, ACT_SETUP[f"gates{B // 2 - 1}"])
                        pool.tensor_tensor(
                            wog[:, par], won[:].unsqueeze(1).to_broadcast([D, NB, D]),
                            gates[:, bass.ds(g * NB, NB), 0:D], ALU.mult).then_inc(wog_ready, 1)
                    elif step == "mix":
                        inverse_deviation(1, now)
                    elif step == "out":
                        inverse_deviation(2, now)
                    elif step == "final":
                        a, r = acc[:, 1 - par], res[:, 1 - par]
                        pool.wait_ge(acc_done[E - 1], before)
                        pool.wait_ge(out_stored[1 - par], stored_count(g, par))
                        for b in range(NB):
                            last = pool.tensor_tensor(
                                r[:, b * TB:(b + 1) * TB], a[:, b * TB:(b + 1) * TB],
                                gates[:, bass.ds((g - 1) * NB + b, 1), D:2 * D].to_broadcast([P, TB, D]), ALU.mult)
                        last.then_inc(acc_free, 1)
                        pool.wait_ge(acc_free, now)
                        pool.tensor_tensor(r, r, x2[:, 1 - par], ALU.add).then_inc(res_ready, 1)

            def stored_count(g, par):
                if isinstance(g, int):
                    return 16 * ((g - 1) // 2 + 1)
                return 8 * (g + 1) if par == 1 else 8 * g

            start_ahead(pool, [eps_added[0], eps_added[1], eps_added[2], *rstd_ready, wog_ready, res_ready])
            for s in out_stored:
                pool.sem_inc(s, 16)
            rounds(pool, one_round)

        @block.scalar
        def _(act):
            act.dma_start(wmod_sb[:], wmod.rearrange("k (j d) -> k j d", d=D)).then_inc(cond_loaded, 16)
            act.dma_start(wq_sb[:], wq).then_inc(qkv_loaded, 16)
            act.dma_start(wk_sb[:], wk).then_inc(qkv_loaded, 16)
            act.dma_start(wvg_sb[:, 0:D], wv).then_inc(qkv_loaded, 16)
            act.dma_start(b1_rows[:], b1.rearrange("e (j p) -> (e j) p", p=P)).then_inc(expert_small_loaded, 16)
            act.dma_start(b2_sb[:], b2).then_inc(expert_small_loaded, 16)
            act.dma_start(wr_sb[:], Wg).then_inc(expert_small_loaded, 16)
            act.dma_start(w1_sb[:], W1.rearrange("e d h -> d e h")).then_inc(w1_loaded, 16)
            act.wait_ge(cond_loaded, 32)
            act.activation(c_sig[:], c_sb[:], ACT.Sigmoid).then_inc(setup_act, 1)
            for i in range(B // 2):
                act.wait_ge(setup_pe, PE_SETUP[f"gates{i}"])
                act.activation(gates[:, 2 * i:2 * i + 2], (hid_ps[i // 2 % 2] if i % 2 == 0 else y_ps[i // 2 % 2])[:],
                               ACT.Copy).then_inc(setup_act, 1)
            act.wait_ge(w1_loaded, 16)
            act.activation(w1_hi[:], w1_sb[:], ACT.Copy).then_inc(setup_act, 1)

            def modulated(out_tile, ps, which, g):
                for b in range(NB):
                    s = slice(b * T, (b + 1) * T)
                    last = act.activation(out_tile[:, s], ps[:, s], ACT.Identity,
                                          scale=modT[:, 2 * which + 1, bass.ds(g * NB + b, 1)],
                                          bias=modT[:, 2 * which, bass.ds(g * NB + b, 1)])
                return last

            def one_round(g, par, front, attention, experts):
                ahead, now, before, older = done(g + 1), done(g), done(g - 1), done(g - 2)
                for step, i in steps(front, attention, experts):
                    if step == "norm1":
                        act.wait_ge(xn_ps, ahead)
                        if isinstance(g, int) and g == -1:
                            act.wait_ge(setup_dve, DVE_SETUP["mod"])
                        wait(act, vg_ps[1], now)
                        modulated(hT, pA, 0, g + 1).then_inc(hT_ready, 1)
                    elif step == "proj":
                        act.wait_ge(k_ps, ahead)
                        wait(act, cross_ps, now)
                        act.activation(qk[:, 1], pC[:], ACT.Sigmoid)
                        wait(act, carried[1], now)
                        act.activation(f[:], pC[:], ACT.Sigmoid, scale=-1.0).then_inc(f_ready, 1)
                        act.wait_ge(q_ps, ahead)
                        act.activation(q_sig[:], pB[:], ACT.Sigmoid).then_inc(q_sig_ready, 1)
                    elif step == "vgate":
                        wait(act, mix_ps, now)
                        wait(act, og_ready, now)
                        for h, ps in enumerate((pD, pA)):
                            vg = ps[:].rearrange("p (c d) -> p c d", c=2)
                            act.wait_ge(vg_ps[h], ahead)
                            act.activation(gate[:, 2 * h:2 * h + 2], vg[:, :, D:2 * D], ACT.Sigmoid)
                            act.activation(v[:, 2 * h:2 * h + 2], vg[:, :, 0:D], ACT.Copy).then_inc(vg_copied[h], 1)
                    elif step == "level" and i == 6:
                        act.wait_ge(level_ps[6], now)
                        act.wait_ge(level_copied[5], now)
                        ps = pD[:, 0:GROUP // 2].rearrange("p (c t) -> p c t", c=NT)
                        act.activation(at[0:32, :, 32:64], ps[0:32, :, 0:32], ACT.Copy)
                        act.activation(at[64:96, :, 96:128], ps[64:96, :, 32:64], ACT.Copy).then_inc(level_copied[6], 1)
                    elif step == "level" and i == 7:
                        act.wait_ge(level_ps[7], now)
                        ps = pA[:, 0:GROUP // 2].rearrange("p (c t) -> p c t", c=NT)
                        act.activation(at[0:64, :, 64:128], ps[0:64], ACT.Copy).then_inc(level_copied[7], 1)
                    elif step == "cross":
                        act.wait_ge(cross_ps, now)
                        act.activation(ct[:], pB[:, 0:NB * P].rearrange("p (b t) -> p b t", b=NB),
                                       ACT.Copy).then_inc(cross_copied, 1)
                    elif step == "norm2":
                        act.wait_ge(on_ps, now)
                        act.activation(onT[:], pD[:], ACT.Copy).then_inc(onT_ready, 1)
                    elif step == "norm3":
                        act.wait_ge(x2n_ps, now)
                        wait(act, up_ps[3][HH - 1], 2 * older)
                        wait(act, h2_lo_ready, older)
                        modulated(h2T[:, par], pB, 1, g).then_inc(h2T_ready, 1)
                        act.wait_ge(h2T_ready, now)
                        act.activation(h2_hi[:, par], h2T[:, par], ACT.Copy).then_inc(h2_hi_ready, 1)
                    elif step == "route":
                        act.wait_ge(lead_ready, now)
                        act.activation(s1[:], lead[:], ACT.Sigmoid)
                        act.activation(s2[:], lead[:], ACT.Sigmoid, scale=-1.0).then_inc(s12_ready, 1)
                    elif step == "turn":
                        act.wait_ge(score_ps, before)
                        act.activation(sT[:], pD[0:E, :], ACT.Copy).then_inc(sT_ready, 1)
                    elif step == "bias":
                        act.wait_ge(bias_ps, before)
                        act.wait_ge(acc_free, older)
                        act.activation(acc[:, 1 - par], pA[:].rearrange("p (c d) -> p c d", c=NT),
                                       ACT.Copy).then_inc(acc_ready, 1)
                    elif step == "up":
                        if i >= 2:
                            act.wait_ge(y_done[i - 2], before)
                        else:
                            wait(act, y_done[i + E - 2], older)
                        for j in range(HH):
                            act.wait_ge(up_ps[i % 4][j], expert_count(i, before))
                            act.activation(hid[:, i % 2, j], hid_ps[j][:], ACT.Relu,
                                           bias=b1T[:, i * HH + j:i * HH + j + 1]).then_inc(hid_ready[i % 4][j], 1)

            act.wait_ge(setup_dve, DVE_SETUP["b1_turned"])
            start_ahead(act, [hT_ready, f_ready, q_sig_ready, *vg_copied, level_copied[6], level_copied[7], cross_copied,
                              onT_ready, h2T_ready, h2_hi_ready, s12_ready, sT_ready, acc_ready],
                        twice=[s for pair in hid_ready for s in pair])
            rounds(act, one_round)

        @block.vector
        def _(dve):
            dve.wait_ge(setup_act, ACT_SETUP["cond_sigmoid"])
            dve.tensor_tensor(c_act[:], c_sb[:], c_sig[:], ALU.mult).then_inc(setup_dve, 1)
            dve.wait_ge(setup_pe, PE_SETUP["cond"])
            dve.tensor_copy(cT[:], pA[:, 0:B]).then_inc(setup_dve, 1)
            dve.wait_ge(setup_pe, PE_SETUP["wg1"])
            dve.tensor_copy(wg1T[:], pD[:, 0:D]).then_inc(setup_dve, 1)
            dve.wait_ge(setup_pe, PE_SETUP["b1"])
            dve.tensor_copy(b1T[:], pD[:, D:D + E * HH]).then_inc(setup_dve, 1)
            dve.wait_ge(setup_pe, PE_SETUP["mod"])
            for w in range(4):
                last = dve.tensor_scalar(modT[:, w], pB[:, w * B:(w + 1) * B], float(w % 2), None, ALU.add)
            last.then_inc(setup_dve, 1)
            dve.wait_ge(setup_pe, PE_SETUP["gate_rows"])
            dve.tensor_copy(g_raw[:], pC[0:B, 0:2 * D]).then_inc(setup_dve, 1)
            dve.wait_ge(setup_dve, DVE_SETUP["gate_raw"])
            dve.tensor_scalar(g_sign[:], g_raw[:], 0.0, 2.0, ALU.is_ge, ALU.mult)
            dve.scalar_tensor_tensor(g_mag[:], g_raw[:], -1.0, g_raw[:], ALU.mult, ALU.max).then_inc(setup_dve, 1)
            dve.wait_ge(setup_dve, DVE_SETUP["gate_parts"])
            dve.tensor_scalar(g_mag[:], g_mag[:], FLOOR, None, ALU.max).then_inc(setup_dve, 1)
            dve.wait_ge(setup_dve, DVE_SETUP["gate_floor"])
            dve.scalar_tensor_tensor(g_rows[:], g_sign[:], 1.0, g_mag[:], ALU.subtract, ALU.mult).then_inc(setup_dve, 1)
            dve.wait_ge(setup_pe, PE_SETUP["wg12"])
            dve.tensor_copy(wvg_sb[:, D:2 * D], pA[:, 0:D]).then_inc(setup_dve, 1)
            dve.wait_ge(out_w_loaded, 32)
            dve.tensor_scalar(won[:], wo_sb[:], nw_sb[:, 0:1], None, ALU.mult).then_inc(setup_dve, 1)

            def statistics(i, src, now):
                for t in range(NT):
                    last = dve.bn_stats(stat[:, i, t], src[:, t])
                last.then_inc(stats_done[i], 1)
                dve.wait_ge(stats_done[i], now)
                dve.memset(idle[:], 0.0)
                for t in range(NT):
                    last = dve.bn_aggr(mean_var[:, i, t], stat[:, i, t])
                last.then_inc(aggr_done[i], 1)

            def normalized(i, out_tile, src, now):
                dve.wait_ge(rstd_ready[i], now)
                for t in range(NT):
                    last = dve.tensor_scalar(out_tile[:, t], src[:, t], mean_var[:, i, t, 0:1],
                                             rstd[:, i, t:t + 1], ALU.subtract, ALU.mult)
                return last

            def compound(m):
                pair = decay[m][:].rearrange("p (b two) -> p b two", two=2)
                return dve.tensor_tensor(decay[m + 1][:], pair[:, :, 0], pair[:, :, 1], ALU.mult)

            def route(g, par, now, older):
                dve.wait_ge(logit_ps, now)
                lead_view = [P, NT, E]
                logits = pC[:, 0:NT * E].rearrange("p (c e) -> p c e", c=NT)
                dve.tensor_reduce(top1[:], logits, AX.X, ALU.max).then_inc(route_step[1], 1)

                def first_of(top, src, picked, s):
                    dve.wait_ge(route_step[s], now)
                    dve.tensor_tensor(eq[:], src, top[:].unsqueeze(2).to_broadcast(lead_view),
                                      ALU.is_equal).then_inc(route_step[s + 1], 1)
                    dve.wait_ge(route_step[s + 1], now)
                    dve.tensor_tensor(cand[:], eq[:], first_wins[:].rearrange("p (c e) -> p c e", c=NT),
                                      ALU.mult).then_inc(route_step[s + 2], 1)
                    dve.wait_ge(route_step[s + 2], now)
                    dve.tensor_reduce(best[:], cand[:], AX.X, ALU.max).then_inc(route_step[s + 3], 1)
                    dve.wait_ge(route_step[s + 3], now)
                    dve.tensor_tensor(picked[:], cand[:], best[:].unsqueeze(2).to_broadcast(lead_view),
                                      ALU.is_equal).then_inc(route_step[s + 4], 1)

                first_of(top1, logits, pick1, 1)
                dve.wait_ge(route_step[5], now)
                dve.scalar_tensor_tensor(rest[:], pick1[:], LOWEST, logits, ALU.mult, ALU.add).then_inc(route_step[6], 1)
                dve.wait_ge(route_step[6], now)
                dve.tensor_reduce(top2[:], rest[:], AX.X, ALU.max).then_inc(route_step[7], 1)
                dve.wait_ge(route_step[7], now)
                dve.tensor_tensor(lead[:], top1[:], top2[:], ALU.subtract).then_inc(lead_ready, 1)
                first_of(top2, rest[:], pick2, 7)
                dve.wait_ge(s12_ready, now)
                dve.tensor_tensor(part[:], pick1[:], s1[:].unsqueeze(2).to_broadcast(lead_view), ALU.mult)
                dve.wait_ge(route_step[11], now)
                dve.tensor_tensor(pick2[:], pick2[:], s2[:].unsqueeze(2).to_broadcast(lead_view),
                                  ALU.mult).then_inc(route_step[12], 1)
                dve.wait_ge(route_step[12], now)
                wait(dve, acc_done[E - 1], older)
                wait(dve, score_ps, older)
                dve.tensor_tensor(score[:, par], part[:], pick2[:], ALU.add).then_inc(score_ready, 1)

            def x_count(g, par):
                if isinstance(g, int):
                    return 16 * ((g + 1) // 2 + 1)
                return 8 * (g + 3) if par == 1 else 8 * (g + 2)

            def one_round(g, par, front, attention, experts):
                ahead, now, before, older = done(g + 1), done(g), done(g - 1), done(g - 2)
                first = isinstance(g, int) and g == 0
                for step, i in steps(front, attention, experts):
                    if step == "stats1":
                        dve.wait_ge(x_loaded[1 - par], x_count(g, par))
                        statistics(0, x_sb[:, 1 - par], ahead)
                    elif step == "norm1":
                        normalized(0, xn, x_sb[:, 1 - par], ahead).then_inc(xn_ready, 1)
                    elif step == "proj":
                        dve.wait_ge(q_sig_ready, ahead)
                        wait(dve, level_ps[0], now)
                        dve.tensor_tensor(qraw[:], pB[:], q_sig[:], ALU.mult).then_inc(q_ready, 1)
                        dve.wait_ge(f_ready, ahead)
                        dve.tensor_scalar(sgn[:], f[:], 0.5, 2.0, ALU.is_equal, ALU.mult).then_inc(sgn_ready, 1)
                        dve.wait_ge(sgn_ready, ahead)
                        dve.scalar_tensor_tensor(decay[0][:], sgn[:], 1.0, f[:], ALU.subtract, ALU.mult).then_inc(a_ready, 1)
                        dve.wait_ge(q_ready, ahead)
                        dve.wait_ge(a_ready, ahead)
                        wait(dve, cross_ps, now)
                        compound(0)
                        dve.tensor_tensor(qk[:, 0], qraw[:], decay[0][:], ALU.mult).then_inc(carried[1], 1)
                    elif step == "diag":
                        if first:
                            dve.wait_ge(setup_pool, POOL_SETUP["ident"])
                            dve.wait_ge(setup_pool, POOL_SETUP["masks"])
                        dve.wait_ge(level_ps[0], now)
                        wait(dve, mix_ps, before)
                        dve.tensor_tensor(at[:], pB[:].rearrange("p (c t) -> p c t", c=NT),
                                          ident[:].unsqueeze(1).to_broadcast([P, NT, P]), ALU.mult).then_inc(level_copied[0], 1)
                    elif step == "level":
                        m = 1 << (i - 1)
                        dve.wait_ge(level_ps[i], now)
                        dve.wait_ge(carried[i], now)
                        if i < LEVELS:
                            if i <= 5:
                                dve.wait_ge(level_copied[i - 1], now)
                            if i < LEVELS - 1:
                                compound(i)
                            blocks = GROUP // (2 * m)
                            part_view = halves(m, m, 0, blocks)
                            over = decay[i - 1][:].rearrange("p (b two) -> p two b", two=2)
                            dve.tensor_tensor(part_view, part_view, over.unsqueeze(3).to_broadcast([D, 2, blocks, m]),
                                              ALU.mult).then_inc(carried[i + 1], 1)
                        else:
                            over = decay[i - 1][:].rearrange("p (b four) -> p b four", four=4)
                            q2 = qk[:, 0].rearrange("p (b c m) -> p b c m", b=NB, c=4)[:, :, 3]
                            k1 = qk[:, 1].rearrange("p (b c m) -> p b c m", b=NB, c=4)[:, :, 0]
                            dve.tensor_tensor(q2, q2, over[:, :, 2:3].to_broadcast([D, NB, m]), ALU.mult)
                            dve.tensor_tensor(k1, k1, over[:, :, 1:2].to_broadcast([D, NB, m]),
                                              ALU.mult).then_inc(carried[8], 1)
                        if i <= 5:
                            blocks = GROUP // (2 * m)
                            dst = at[:].rearrange("p c t -> p (c t)").rearrange("p (b two m) -> p b two m", two=2, m=m)[:, :, 1]
                            src = LEVEL_BANK[i][:, 0:GROUP // 2].rearrange("p (b m) -> p b m", m=m)
                            msk = level_mask[:, i - 1].bitcast(I32).rearrange("p (b m) -> p b m", m=m)
                            dve.copy_predicated(dst, msk, src).then_inc(level_copied[i], 1)
                    elif step == "mix":
                        dve.wait_ge(mix_ps, now)
                        dve.scalar_tensor_tensor(og[:], pC[:].rearrange("p (c d) -> p c d", c=NT), QSCALE, gate[:],
                                                 ALU.mult, ALU.mult).then_inc(og_ready, 1)
                        dve.wait_ge(og_ready, now)
                        statistics(1, og, now)
                    elif step == "norm2":
                        normalized(1, on, og, now).then_inc(on_ready, 1)
                    elif step == "out":
                        dve.wait_ge(out_ps, now)
                        wait(dve, res_ready, older)
                        dve.tensor_tensor(x2[:, par], pA[:].rearrange("p (c d) -> p c d", c=NT), x_sb[:, par],
                                          ALU.add).then_inc(x2_ready, 1)
                        dve.wait_ge(x2_ready, now)
                        statistics(2, x2[:, par], now)
                    elif step == "norm3":
                        normalized(2, x2n, x2[:, par], now).then_inc(x2n_ready, 1)
                        dve.wait_ge(h2_hi_ready, now)
                        dve.tensor_tensor(h2_lo[:, par], h2T[:, par], h2_hi[:, par].bitcast(F32),
                                          ALU.subtract).then_inc(h2_lo_ready, 1)
                    elif step == "route":
                        route(g, par, now, older)
                    elif step == "down":
                        dve.wait_ge(y_done[i], before)
                        dve.wait_ge(acc_ready if i == 0 else acc_done[i - 1], before)
                        if i == 0:
                            dve.wait_ge(score_ready, before)
                        for t in range(NT):
                            a = acc[:, 1 - par, t]
                            last = dve.scalar_tensor_tensor(a, y_ps[i % 2][:, t], score[:, 1 - par, t, i:i + 1], a,
                                                            ALU.mult, ALU.add)
                        last.then_inc(acc_done[i], 1)
                if first:
                    dve.wait_ge(setup_act, ACT_SETUP["w1_hi"])
                    dve.tensor_tensor(w1_lo[:], w1_sb[:], w1_hi[:].bitcast(F32), ALU.subtract).then_inc(setup_dve, 1)

            start_ahead(dve, [*stats_done, *aggr_done, xn_ready, q_ready, sgn_ready, a_ready, og_ready, on_ready,
                              x2_ready, x2n_ready, h2_lo_ready, lead_ready, score_ready, *level_copied[:6],
                              *carried.values(), *route_step.values(), *acc_done])
            rounds(dve, one_round)

        @block.tensor
        def _(pe):
            def mm(o, lhsT, rhs, start=True, stop=True):
                return pe.matmul(o, lhsT, rhs, start=start, stop=stop)

            pe.wait_ge(setup_pool, POOL_SETUP["ident"])
            pe.wait_ge(setup_dve, DVE_SETUP["cond_act"])
            pe.transpose(pA[:, 0:B], c_act[:], ident[0:B, 0:B]).then_inc(setup_pe, 1)
            pe.wait_ge(gate_w_loaded, 32)
            pe.transpose(pD[:, 0:D], wg1_sb[:], ident[:]).then_inc(setup_pe, 1)
            pe.wait_ge(expert_small_loaded, 48)
            pe.wait_ge(setup_dve, DVE_SETUP["wg1_turned"])
            pe.transpose(pD[:, D:D + E * HH], b1_rows[:], ident[0:E * HH, 0:E * HH]).then_inc(setup_pe, 1)
            pe.wait_ge(setup_dve, DVE_SETUP["cond_turned"])
            for w, j in enumerate((0, 1, 3, 4)):
                last = mm(pB[:, w * B:(w + 1) * B], wmod_sb[:, j], cT[:])
            last.then_inc(setup_pe, 1)
            mm(pC[0:B, 0:D], cT[:], wmod_sb[:, 2])
            mm(pC[0:B, D:2 * D], cT[:], wmod_sb[:, 5]).then_inc(setup_pe, 1)
            mm(pA[:, 0:D], wg1T[:], wg2_sb[:]).then_inc(setup_pe, 1)
            pe.wait_ge(setup_dve, DVE_SETUP["gate_rows"])
            for i in range(B // 2):
                ps = (hid_ps[i // 2 % 2][:] if i % 2 == 0 else y_ps[i // 2 % 2][:].rearrange("p c d -> p (c d)"))
                if i >= 4:
                    pe.wait_ge(setup_act, ACT_SETUP[f"gates{i - 4}"])
                for b in range(2):
                    pick = ident[0:B, 2 * i + b:2 * i + b + 1].to_broadcast([B, P])
                    last = mm(ps[:, b * 2 * D:(b + 1) * 2 * D], pick, g_rows[:])
                last.then_inc(setup_pe, 1)

            def turn(ps, src):
                for t in range(NT):
                    last = pe.transpose(ps[:, t * P:(t + 1) * P], src[:, t], ident[:])
                return last

            def one_round(g, par, front, attention, experts):
                ahead, now, before, older = done(g + 1), done(g), done(g - 1), done(g - 2)
                first = isinstance(g, int) and g == -1
                for step, i in steps(front, attention, experts):
                    if step == "norm1":
                        pe.wait_ge(xn_ready, ahead)
                        if first:
                            pe.wait_ge(setup_dve, DVE_SETUP["wg12"])
                        wait(pe, level_copied[7], now)
                        turn(pA, xn).then_inc(xn_ps, 1)
                    elif step == "proj":
                        pe.wait_ge(hT_ready, ahead)
                        if first:
                            pe.wait_ge(qkv_loaded, 48)
                            pe.wait_ge(setup_dve, DVE_SETUP["mod"])
                            pe.wait_ge(setup_dve, DVE_SETUP["gate_raw"])
                        wait(pe, h2T_ready, now)
                        mm(pB[:], wq_sb[:], hT[:]).then_inc(q_ps, 1)
                        wait(pe, og_ready, now)
                        mm(pC[:], wk_sb[:], hT[:]).then_inc(k_ps, 1)
                    elif step == "vgate":
                        if first:
                            pe.wait_ge(setup_dve, DVE_SETUP["b1_turned"])
                        for h, ps in enumerate((pD, pA)):
                            wait(pe, onT_ready if h == 0 else x2_ready, now)
                            for t in range(2):
                                tok = slice((2 * h + t) * P, (2 * h + t + 1) * P)
                                last = mm(ps[:, t * 2 * D:(t + 1) * 2 * D], hT[:, tok], wvg_sb[:])
                            last.then_inc(vg_ps[h], 1)
                    elif step == "diag":
                        pe.wait_ge(q_ready, now)
                        pe.wait_ge(f_ready, now)
                        for t in range(NT):
                            tok = slice(t * P, (t + 1) * P)
                            last = mm(pB[:, tok], qk[:, 1, tok], qraw[:, tok])
                        last.then_inc(level_ps[0], 1)
                    elif step == "level":
                        m = 1 << (i - 1)
                        pe.wait_ge(carried[i], now)
                        if i == 1:
                            pe.wait_ge(f_ready, now)
                            wait(pe, lead_ready, before)
                        elif i in (2, 3):
                            if experts:
                                pe.wait_ge(sT_ready if i == 2 else acc_ready, before)
                            else:
                                pe.wait_ge(vg_copied[i - 2], now)
                        else:
                            pe.wait_ge(level_copied[i - 4], now)
                        rows = {6: 96, 7: 64}.get(i, P)
                        for t in range(NT):
                            tok = slice(t * P, (t + 1) * P)
                            q_second = qk[:, 0, tok].rearrange("p (b two m) -> p b two m", two=2, m=m)[:, :, 1]
                            last = mm(LEVEL_BANK[i][0:rows, t * P // 2:(t + 1) * P // 2].rearrange("p (b m) -> p b m", m=m),
                                      qk[:, 1, t * P:t * P + rows], q_second)
                        last.then_inc(level_ps[i], 1)
                    elif step == "cross":
                        pe.wait_ge(carried[8], now)
                        pe.wait_ge(level_copied[4], now)
                        for b in range(NB):
                            s, t = slice(2 * b * P, (2 * b + 1) * P), slice((2 * b + 1) * P, (2 * b + 2) * P)
                            last = mm(pB[:, b * P:(b + 1) * P], qk[:, 1, s], qk[:, 0, t])
                        last.then_inc(cross_ps, 1)
                    elif step == "mix":
                        pe.wait_ge(vg_copied[1], now)
                        pe.wait_ge(level_copied[5], now)
                        pe.wait_ge(cross_copied, now)
                        for t in range(NT):
                            o = pC[:, t * D:(t + 1) * D]
                            later = t % TB == 1
                            last = mm(o, at[:, t], v[:, t], stop=not later)
                            if later:
                                last = mm(o, ct[:, t // TB], v[:, t - 1], start=False)
                        last.then_inc(mix_ps, 1)
                    elif step == "norm2":
                        pe.wait_ge(on_ready, now)
                        pe.wait_ge(level_copied[6], now)
                        turn(pD, on).then_inc(on_ps, 1)
                    elif step == "out":
                        pe.wait_ge(onT_ready, now)
                        pe.wait_ge(wog_ready, now)
                        pe.wait_ge(hT_ready, ahead) if front else pe.wait_ge(level_copied[7], now)
                        for t in range(NT):
                            last = mm(pA[:, t * D:(t + 1) * D], onT[:, t * P:(t + 1) * P], wog[:, par, t // TB])
                        last.then_inc(out_ps, 1)
                    elif step == "norm3":
                        pe.wait_ge(x2n_ready, now)
                        turn(pB, x2n).then_inc(x2n_ps, 1)
                    elif step == "route":
                        pe.wait_ge(h2T_ready, now)
                        pe.wait_ge(f_ready, ahead) if front else pe.wait_ge(og_ready, now)
                        for t in range(NT):
                            last = mm(pC[:, t * E:(t + 1) * E], h2T[:, par, t * P:(t + 1) * P], wr_sb[:])
                        last.then_inc(logit_ps, 1)
                    elif step == "turn":
                        pe.wait_ge(score_ready, before)
                        pe.wait_ge(vg_copied[0], now) if attention else pe.wait_ge(onT_ready, before)
                        for t in range(NT):
                            last = pe.transpose(pD[0:E, t * P:(t + 1) * P], score[:, 1 - par, t], ident[:])
                        last.then_inc(score_ps, 1)
                    elif step == "bias":
                        pe.wait_ge(sT_ready, before)
                        pe.wait_ge(vg_copied[1], now) if attention else pe.wait_ge(x2_ready, before)
                        for t in range(NT):
                            last = mm(pA[:, t * D:(t + 1) * D], sT[:, t * P:(t + 1) * P], b2_sb[:])
                        last.then_inc(bias_ps, 1)
                    elif step == "up":
                        if i == 0:
                            pe.wait_ge(h2_lo_ready, before)
                            if isinstance(g, int) and g == 1 or not isinstance(g, int):
                                pe.wait_ge(setup_dve, DVE_SETUP["w1_lo"])
                        x_hi, x_lo = h2_hi[:, 1 - par], h2_lo[:, 1 - par]
                        for j in range(HH):
                            if i >= 1:
                                pe.wait_ge(hid_ready[(i - 1) % 4][j], expert_count(i - 1, before))
                            else:
                                wait(pe, hid_ready[3][j], 2 * older)
                            w = slice(j * P, (j + 1) * P)
                            mm(hid_ps[j][:], w1_hi[:, i, w], x_hi, stop=False)
                            mm(hid_ps[j][:], w1_hi[:, i, w], x_lo, start=False, stop=False)
                            mm(hid_ps[j][:], w1_lo[:, i, w], x_hi, start=False).then_inc(up_ps[i % 4][j], 1)
                    elif step == "down":
                        if i == 0:
                            pe.wait_ge(w2_loaded, 16)
                        pe.wait_ge(hid_ready[i % 4][HH - 1], expert_count(i, before))
                        if i >= 2:
                            pe.wait_ge(acc_done[i - 2], before)
                        else:
                            wait(pe, acc_done[i + E - 2], older)
                        for t in range(NT):
                            for j in range(HH):
                                last = mm(y_ps[i % 2][:, t], hid[:, i % 2, j, t * P:(t + 1) * P], w2_sb[:, i, j],
                                          start=j == 0, stop=j == HH - 1)
                        last.then_inc(y_done[i], 1)

            pe.wait_ge(setup_act, ACT_SETUP[f"gates{B // 2 - 1}"])
            start_ahead(pe, [xn_ps, q_ps, k_ps, on_ps, out_ps, x2n_ps, logit_ps, score_ps, bias_ps, cross_ps, mix_ps,
                             *vg_ps, *level_ps, *y_done],
                        twice=[s for pair in up_ps for s in pair])
            rounds(pe, one_round)


_INS = ["L0_attn_x", "L0_attn_wq", "L0_attn_wk", "L0_attn_wv", "L0_attn_wo", "L0_attn_wg1", "L0_attn_wg2",
        "L0_attn_norm_w", "L0_ffn_Wg", "L0_ffn_W1", "L0_ffn_b1", "L0_ffn_W2", "L0_ffn_b2", "L0_c", "L0_wmod"]


def kernel(**inputs):
    import numpy as _np
    import concourse.bacc as _bacc
    from concourse import mybir as _mybir
    from concourse.bass_utils import run_bass_kernel_spmd as _run

    nc = _bacc.Bacc("TRN2", target_bir_lowering=False, num_devices=1)
    arrays, args = {}, []
    for name in _INS:
        a = _np.ascontiguousarray(inputs[name])
        arrays[f"in_{name}_dram"] = a
        args.append(nc.dram_tensor(f"in_{name}_dram", a.shape, _mybir.dt.from_np(a.dtype), kind="ExternalInput").ap())
    shape = tuple(inputs["L0_attn_x"].shape)
    out = nc.dram_tensor("out_0_dram", shape, _mybir.dt.float32, kind="ExternalOutput").ap()
    adaln_block_kernel(nc, *args, out)
    r = _run(nc, [arrays], core_ids=[0])
    return r.results[0]["out_0_dram"]
```

```python
from contextlib import ExitStack

import concourse.bass as bass
from concourse import mybir

ALU = mybir.AluOpType
ACT = mybir.ActivationFunctionType
AX = mybir.AxisListType
F32 = mybir.dt.float32
F32R = mybir.dt.float32r
I32 = mybir.dt.int32

P = 128
EPS = 1e-5
FLOOR = 0.25
LOWEST = -3.0e38

FRONT = {"stats1", "norm1", "keys", "queries", "decays", "vgate"}
EXPERTS = {"up", "relu", "turn", "bias", "spread", "weigh", "round", "rest", "down", "final", "back", "add"}
ORDER = [
    ("diag", 0), ("wog", 0), ("up", 0), ("level", 1), ("relu", 0), ("turn", 0), ("up", 1), ("relu", 1),
    ("spread", 0), ("weigh", 0), ("round", 0), ("level", 2), ("up", 2), ("relu", 2), ("spread", 1),
    ("weigh", 1), ("bias", 0), ("level", 3), ("round", 1), ("rest", 0), ("up", 3), ("spread", 2), ("rest", 1),
    ("level", 4), ("relu", 3), ("weigh", 2), ("up", 4), ("down", 0), ("relu", 4), ("stats1", 0),
    ("spread", 3), ("level", 5), ("weigh", 3), ("down", 1), ("round", 2), ("round", 3), ("level", 6),
    ("rest", 2), ("up", 5), ("rest", 3), ("level", 7), ("down", 2), ("spread", 4), ("relu", 5), ("cross", 0),
    ("norm1", 0), ("weigh", 4), ("mix", 0), ("spread", 5), ("weigh", 5), ("up", 6), ("relu", 6), ("down", 3),
    ("up", 7), ("round", 4), ("round", 5), ("spread", 6), ("norm2", 0), ("relu", 7), ("rest", 4), ("keys", 0),
    ("rest", 5), ("weigh", 6), ("out", 0), ("queries", 0), ("spread", 7), ("down", 4), ("weigh", 7),
    ("down", 5), ("round", 6), ("round", 7), ("vgate", 0), ("vgate", 1), ("rest", 6), ("down", 6),
    ("norm3", 0), ("rest", 7), ("decays", 0), ("down", 7), ("h2_lo", 0), ("final", 0), ("route", 0),
    ("back", 0), ("add", 0),
]
FIRST_ORDER = [
    ("diag", 0), ("level", 1), ("level", 2), ("stats1", 0), ("level", 3), ("level", 4), ("level", 5),
    ("level", 6), ("level", 7), ("cross", 0), ("norm1", 0), ("mix", 0), ("gates", 0), ("wog", 0),
    ("gates", 1), ("gates", 2), ("norm2", 0), ("out", 0), ("gates", 3), ("keys", 0), ("queries", 0),
    ("vgate", 0), ("norm3", 0), ("decays", 0), ("h2_lo", 0), ("vgate", 1), ("route", 0),
]
LAST_ORDER = [
    ("up", 0), ("relu", 0), ("up", 1), ("turn", 0), ("spread", 0), ("bias", 0), ("relu", 1), ("up", 2),
    ("weigh", 0), ("relu", 2), ("spread", 1), ("weigh", 1), ("round", 0), ("up", 3), ("spread", 2),
    ("relu", 3), ("rest", 0), ("up", 4), ("down", 0), ("weigh", 2), ("round", 1), ("spread", 3), ("relu", 4),
    ("rest", 1), ("weigh", 3), ("down", 1), ("spread", 4), ("round", 2), ("up", 5), ("rest", 2), ("weigh", 4),
    ("round", 3), ("down", 2), ("relu", 5), ("round", 4), ("spread", 5), ("rest", 3), ("up", 6), ("down", 3),
    ("weigh", 5), ("rest", 4), ("relu", 6), ("round", 5), ("spread", 6), ("up", 7), ("down", 4), ("weigh", 6),
    ("spread", 7), ("rest", 5), ("relu", 7), ("down", 5), ("weigh", 7), ("round", 6), ("round", 7),
    ("rest", 6), ("rest", 7), ("down", 6), ("down", 7), ("final", 0), ("back", 0), ("add", 0),
]


def adaln_block_kernel(nc, x, wq, wk, wv, wo, wg1, wg2, norm_w, Wg, W1, b1, W2, b2, c, wmod, out):
    B, T, D = x.shape
    E, _, H = W1.shape
    GROUP = 512
    NG = B * T // GROUP
    NB = GROUP // T
    NT = GROUP // P
    TB = T // P
    HH = H // P
    LEVELS = 7
    assert D == P and T == 2 * P and HH == 2 and NG % 2 == 0 and B <= P and E * HH <= P and E == 8 and B % 4 == 0
    QSCALE = float(2 * D) ** -0.5

    xg = x.rearrange("b t d -> (b t) d").rearrange("(g c p) d -> g p c d", p=P, c=NT)
    outg = out.rearrange("b t d -> (b t) d").rearrange("(g c p) d -> g p c d", p=P, c=NT)

    with ExitStack() as ctx:
        def sb(name, shape, dt=F32):
            return ctx.enter_context(nc.sbuf_tensor(name, shape, dt))

        def sem(name):
            return ctx.enter_context(nc.semaphore(name))

        def sems(name, n):
            return [sem(f"{name}{i}") for i in range(n)]

        hid_ps = [ctx.enter_context(nc.psum_tensor(f"hid_ps{i}", [P, GROUP], F32)) for i in range(HH)]
        sum_ps, spread_ps = (ctx.enter_context(nc.psum_tensor(n, [P, GROUP], F32)) for n in ("sum_ps", "spread_ps"))
        pA, pB, pC, pD = [ctx.enter_context(nc.psum_tensor(f"p{n}", [P, GROUP], F32)) for n in "ABCD"]
        LEVEL_BANK = [pB, pC, pD, pA, pB, pC, pD, pA]

        ident = sb("ident", [P, P])
        level_mask = sb("level_mask", [P, 5, P // 2])
        idle = sb("idle", [P, 1])
        ones = sb("ones", [P, P // 2])
        minus_half = sb("minus_half", [P, NT])
        eps4 = sb("eps4", [P, NT])
        first_wins = sb("first_wins", [P, NT * E])
        w_in = sb("w_in", [D, 4, D])
        w_in_hi, w_in_lo = sb("w_in_hi", [D, 4, D], F32R), sb("w_in_lo", [D, 4, D], F32R)
        wg1_sb, wg2_sb, wg1T = sb("wg1_sb", [D, D]), sb("wg2_sb", [D, D]), sb("wg1T", [D, D])
        wo_sb, won = sb("wo_sb", [D, D]), sb("won", [D, D])
        nw_sb = sb("nw_sb", [D, 1])
        wr_sb = sb("wr_sb", [D, E])
        PARTS = 2 * 32 + E
        b2_in = sb("b2_in", [PARTS, D])
        b2_hi, b2_parts = sb("b2_hi", [PARTS, D], F32R), sb("b2_parts", [PARTS, D], F32R)
        pick = sb("pick", [PARTS, E], F32R)
        b1_rows, b1T = sb("b1_rows", [E * HH, P]), sb("b1T", [P, E * HH])
        w1_sb = sb("w1_sb", [D, E, H])
        w1_hi, w1_lo = sb("w1_hi", [D, E, H], F32R), sb("w1_lo", [D, E, H], F32R)
        w2_sb = sb("w2_sb", [P, E, HH, D])
        w2_hi, w2_lo = sb("w2_hi", [P, E, HH, D], F32R), sb("w2_lo", [P, E, HH, D], F32R)
        c_sb, c_sig, c_act, cT = sb("c_sb", [B, D]), sb("c_sig", [B, D]), sb("c_act", [B, D]), sb("cT", [D, B])
        wmod_sb = sb("wmod_sb", [D, 6, D])
        modT = sb("modT", [D, 4, B])
        ga_work = [sb(f"ga_{n}", [B, D]) for n in ("raw", "sign", "mag", "rows")]
        gb_work = [sb(f"gb_{n}", [D, B]) for n in ("raw", "sign", "mag", "columns")]
        ga_rows, gbT = ga_work[3], gb_work[3]
        gates = sb("gates", [P, B, D])
        x_sb, x2, res = (sb(n, [P, 2, NT, D]) for n in ("x_sb", "x2", "res"))
        wog = sb("wog", [D, 2, NB, D])
        h2T = sb("h2T", [D, 2, GROUP])
        h2_hi, h2_lo = sb("h2_hi", [D, 2, GROUP], F32R), sb("h2_lo", [D, 2, GROUP], F32R)
        score_parts = sb("score_parts", [P, 2, NT, PARTS], F32R)
        stat = sb("stat", [P, 3, NT, 6])
        mean_var = sb("mean_var", [P, 3, NT, 2])
        var_eps, rstd = sb("var_eps", [P, 3, NT]), sb("rstd", [P, 3, NT])
        xn, on, x2n, og = (sb(n, [P, NT, D]) for n in ("xn", "on", "x2n", "og"))
        hT, onT = sb("hT", [D, GROUP]), sb("onT", [D, GROUP])
        hT_hi, hT_lo = sb("hT_hi", [D, GROUP], F32R), sb("hT_lo", [D, GROUP], F32R)
        q_sig, qraw, f, sgn = (sb(n, [D, GROUP]) for n in ("q_sig", "qraw", "f", "sgn"))
        qk = sb("qk", [D, 2, GROUP])
        decay = [sb(f"decay{m}", [D, GROUP >> m]) for m in range(LEVELS)]
        gate, v = sb("gate", [P, NT, D]), sb("v", [P, NT, D])
        at = sb("at", [P, NT, P])
        ct = sb("ct", [P, NB, P])
        score = sb("score", [P, NT, E])
        sT = sb("sT", [PARTS, GROUP], F32R)
        hid, weighted = sb("hid", [P, 2, HH, GROUP]), sb("weighted", [P, 2, HH, GROUP])
        w_hid_hi, w_hid_lo = (sb(n, [P, 2, HH, GROUP], F32R) for n in ("w_hid_hi", "w_hid_lo"))
        sumT = sb("sumT", [D, GROUP])
        eq, cand, pick1, rest, pick2, part = (
            sb(n, [P, NT, E]) for n in ("eq", "cand", "pick1", "rest", "pick2", "part"))
        top1, top2, best, lead, s1, s2 = (sb(n, [P, NT]) for n in ("top1", "top2", "best", "lead", "s1", "s2"))

        x_loaded, out_stored = sems("x_loaded", 2), sems("out_stored", 2)
        (c_loaded, cond_loaded, gate_w_loaded, qkv_loaded, out_w_loaded, b1_loaded, router_loaded, b2_loaded,
         w1_loaded, w2_loaded) = map(sem, (
            "c_loaded", "cond_loaded", "gate_w_loaded", "qkv_loaded", "out_w_loaded", "b1_loaded", "router_loaded",
            "b2_loaded", "w1_loaded", "w2_loaded"))
        setup_pool, setup_act, setup_dve, setup_pe = map(sem, ("setup_pool", "setup_act", "setup_dve", "setup_pe"))
        POOL_SETUP = {name: n + 1 for n, name in enumerate(
            ["memsets", "ident", "mask0", "mask1", "mask2", "mask3", "mask4", "masks", "w1_lo", "w2_lo"])}
        ACT_SETUP = {name: n + 1 for n, name in enumerate(
            ["cond_sigmoid", "w_in_hi", "w1_hi", "b2_hi", "w2_hi"] + [f"gates{i}" for i in range(B // 4)])}
        DVE_SETUP = {name: n + 1 for n, name in enumerate(
            ["cond_act", "cond_turned", "wg1_turned", "mod", "wg12", "w_in_lo", "gate_raw", "gate_parts", "gate_floor",
             "gates", "won", "pick", "b2_parts"])}
        PE_SETUP = {name: n + 1 for n, name in enumerate(
            ["cond", "wg1", "mod", "wg12", "gate_rows"] + [f"gates{i}" for i in range(B // 4)])}
        stats_done, aggr_done, eps_added, rstd_ready = (
            sems(n, 3) for n in ("stats_done", "aggr_done", "eps_added", "rstd_ready"))
        (xn_ready, xn_ps, hT_ready, hT_hi_ready, hT_lo_ready, q_ps, k_ps, f_ready, q_sig_ready, q_ready, sgn_ready, a_ready,
         og_ready, on_ready, on_ps, onT_ready, out_ps, x2_ready, x2n_ready, x2n_ps, h2T_ready, h2_hi_ready,
         h2_lo_ready, logit_ps, lead_ready, s12_ready, score_sum, score_hi_ready, score_ready,
         score_ps, sT_ready, cross_ps, cross_copied, mix_ps, wog_ready, sum_taken, back_ps, res_ready) = map(sem, (
            "xn_ready", "xn_ps", "hT_ready", "hT_hi_ready", "hT_lo_ready", "q_ps", "k_ps", "f_ready", "q_sig_ready",
            "q_ready", "sgn_ready", "a_ready", "og_ready", "on_ready", "on_ps", "onT_ready", "out_ps", "x2_ready", "x2n_ready", "x2n_ps",
            "h2T_ready", "h2_hi_ready", "h2_lo_ready", "logit_ps", "lead_ready", "s12_ready", "score_sum",
            "score_hi_ready", "score_ready", "score_ps", "sT_ready", "cross_ps", "cross_copied", "mix_ps", "wog_ready",
            "sum_taken", "back_ps", "res_ready"))
        vg_ps, vg_copied = sems("vg_ps", 2), sems("vg_copied", 2)
        level_ps, level_copied = sems("level_ps", 8), sems("level_copied", 8)
        carried = dict(enumerate(sems("carried", 8), 1))
        route_step = dict(enumerate(sems("route_step", 12), 1))
        up_ps, hid_ready, rest_ready = sems("up_ps", HH), sems("hid_ready", HH), sems("rest_ready", HH)
        spread_done, weighted_ready, rounded, down_done = map(sem, (
            "spread_done", "weighted_ready", "rounded", "down_done"))

        def done(group):
            return group + 2

        def expert_count(e, groups):
            return E * groups - (E - 1 - e)

        def wait(eng, semaphore, count):
            if not isinstance(count, int) or count > 1:
                eng.wait_ge(semaphore, count)

        def wait_expert(eng, semaphore, e, groups):
            count = expert_count(e, groups)
            if not isinstance(count, int) or count > E:
                eng.wait_ge(semaphore, count)

        def start_ahead(eng, by_group, by_expert=()):
            for s in by_group:
                eng.sem_inc(s, 1)
            for s in by_expert:
                eng.sem_inc(s, E)

        def rounds(eng, one_round):
            one_round(-1, 1, front=True, attention=False, experts=False)
            one_round(0, 0, front=True, attention=True, experts=False)
            with eng.Fori(0, NG // 2 - 1) as j:
                one_round(2 * j + 1, 1, front=True, attention=True, experts=True)
                one_round(2 * j + 2, 0, front=True, attention=True, experts=True)
            one_round(NG - 1, 1, front=False, attention=True, experts=True)
            one_round(NG, 0, front=False, attention=False, experts=True)

        def steps(front, attention, experts):
            if attention and not experts:
                return FIRST_ORDER
            if not attention and experts:
                return LAST_ORDER
            return [(s, i) for s, i in ORDER
                    if (front if s in FRONT else experts if s in EXPERTS else attention)]

        gates_bank = [hid_ps[0], hid_ps[1], sum_ps, spread_ps]
        assert B // 4 == len(gates_bank)

        def halves(m, first_q, first_k, blocks):
            base = qk[:]
            return bass.AP(tensor=base.tensor, offset=first_q,
                           ap=[list(base.ap[0]), [GROUP + first_k - first_q, 2], [2 * m, blocks], [1, m]])

        block = ctx.enter_context(nc.Block())

        @block.sync
        def _(sp):
            sp.dma_start(c_sb[:], c).then_inc(c_loaded, 16)
            sp.dma_start(x_sb[:, 0], xg[0]).then_inc(x_loaded[0], 16)
            sp.dma_start(wg1_sb[:], wg1).then_inc(gate_w_loaded, 16)
            sp.dma_start(wg2_sb[:], wg2).then_inc(gate_w_loaded, 16)
            sp.dma_start(b1_rows[:], b1.rearrange("e (j p) -> (e j) p", p=P)).then_inc(b1_loaded, 16)
            sp.dma_start(w_in[:, 0], wq).then_inc(qkv_loaded, 16)
            sp.dma_start(w_in[:, 1], wk).then_inc(qkv_loaded, 16)
            sp.dma_start(w_in[:, 2], wv).then_inc(qkv_loaded, 16)
            sp.dma_start(x_sb[:, 1], xg[1]).then_inc(x_loaded[1], 16)
            sp.dma_start(wo_sb[:], wo).then_inc(out_w_loaded, 16)
            sp.dma_start(nw_sb[:], norm_w.rearrange("(p a) -> p a", a=1)).then_inc(out_w_loaded, 16)
            sp.dma_start(w1_sb[:], W1.rearrange("e d h -> d e h")).then_inc(w1_loaded, 16)
            sp.dma_start(wr_sb[:], Wg).then_inc(router_loaded, 16)
            sp.wait_ge(setup_pool, POOL_SETUP["memsets"])
            for row in (0, 32, 64):
                sp.dma_start(b2_in[row:row + E], b2).then_inc(b2_loaded, 16)
            sp.dma_start(w2_sb[:], W2.rearrange("e (j p) d -> p e j d", p=P)).then_inc(w2_loaded, 16)

            def one_round(g, par, front, attention, experts):
                if front and not (isinstance(g, int) and g < 1):
                    sp.wait_ge(x2_ready, done(g - 1))
                    sp.dma_start(x_sb[:, 1 - par], xg[g + 1]).then_inc(x_loaded[1 - par], 16)
                if experts:
                    sp.wait_ge(res_ready, done(g - 1))
                    sp.dma_start(outg[g - 1], res[:, 1 - par]).then_inc(out_stored[1 - par], 16)

            rounds(sp, one_round)
            for s in out_stored:
                sp.wait_ge(s, 16 * (NG // 2 + 1))

        @block.gpsimd
        def _(pool):
            pool.memset(ident[:], 0.0)
            pool.memset(ones[:], 1.0)
            pool.memset(minus_half[:], -0.5)
            pool.memset(eps4[:], EPS)
            pool.memset(b2_in[:], 0.0)
            pool.memset(score_parts[:].bitcast(F32), 0.0)
            pool.iota(first_wins[:], pattern=[[0, NT], [-1, E]], base=E, channel_multiplier=0,
                      allow_small_or_imprecise_dtypes=True).then_inc(setup_pool, 1)
            pool.wait_ge(setup_pool, POOL_SETUP["memsets"])
            pool.affine_select(out=ident[:], in_=ident[:], compare_op=ALU.not_equal, fill=1.0, base=0,
                               pattern=[[-1, P]], channel_multiplier=1).then_inc(setup_pool, 1)
            def masks():
                for i in range(5):
                    m = 1 << i
                    blocks = P // (2 * m)
                    mask = level_mask[:, i].rearrange("p (b m) -> p b m", m=m)
                    pool.affine_select(out=mask, in_=ones[:].rearrange("p (b m) -> p b m", m=m),
                                       compare_op=ALU.is_ge, fill=0.0, base=0,
                                       pattern=[[-2 * m, blocks], [0, m]],
                                       channel_multiplier=1).then_inc(setup_pool, 1)
                    pool.wait_ge(setup_pool, POOL_SETUP[f"mask{i}"])
                    last = pool.affine_select(out=mask, in_=mask, compare_op=ALU.is_ge, fill=0.0, base=m - 1,
                                              pattern=[[2 * m, blocks], [0, m]], channel_multiplier=-1)
                last.then_inc(setup_pool, 1)

            def inverse_deviation(i, now):
                pool.wait_ge(aggr_done[i], now)
                pool.tensor_tensor(var_eps[:, i], mean_var[:, i, :, 1], eps4[:], ALU.add).then_inc(eps_added[i], 1)
                pool.wait_ge(eps_added[i], now)
                pool.tensor_tensor(rstd[:, i], var_eps[:, i], minus_half[:], ALU.pow).then_inc(rstd_ready[i], 1)

            def one_round(g, par, front, attention, experts):
                ahead, now, before, older = done(g + 1), done(g), done(g - 1), done(g - 2)
                for step, i in steps(front, attention, experts):
                    if step == "stats1":
                        inverse_deviation(0, ahead)
                    elif step == "wog":
                        wait(pool, out_ps, older)
                        if isinstance(g, int) and g == 0:
                            pool.wait_ge(setup_dve, DVE_SETUP["won"])
                            pool.wait_ge(setup_act, ACT_SETUP["gates0"])
                        pool.tensor_tensor(
                            wog[:, par], won[:].unsqueeze(1).to_broadcast([D, NB, D]),
                            gates[:, bass.ds(g * NB, NB)], ALU.mult).then_inc(wog_ready, 1)
                    elif step == "diag" and isinstance(g, int) and g == 0:
                        pool.wait_ge(setup_act, ACT_SETUP["w1_hi"])
                        pool.tensor_tensor(w1_lo[:], w1_sb[:], w1_hi[:].bitcast(F32),
                                           ALU.subtract).then_inc(setup_pool, 1)
                    elif step == "norm1":
                        pool.wait_ge(hT_hi_ready, ahead)
                        wait(pool, vg_ps[1], now)
                        pool.tensor_tensor(hT_lo[:], hT[:], hT_hi[:].bitcast(F32), ALU.subtract).then_inc(hT_lo_ready, 1)
                        if isinstance(g, int) and g == -1:
                            masks()
                    elif step == "mix":
                        inverse_deviation(1, now)
                    elif step == "out":
                        inverse_deviation(2, now)
                    elif step == "norm3" and isinstance(g, int) and g == 0:
                        pool.wait_ge(setup_act, ACT_SETUP["w2_hi"])
                        pool.tensor_tensor(w2_lo[:], w2_sb[:], w2_hi[:].bitcast(F32),
                                           ALU.subtract).then_inc(setup_pool, 1)
                    elif step == "rest":
                        pool.wait_ge(rounded, expert_count(i, before))
                        pool.tensor_tensor(w_hid_lo[:, i % 2, 0], weighted[:, i % 2, 0], w_hid_hi[:, i % 2, 0].bitcast(F32),
                                           ALU.subtract).then_inc(rest_ready[0], 1)
                if isinstance(g, int) and g == 0:
                    pool.wait_ge(setup_act, ACT_SETUP[f"gates{B // 4 - 1}"])

            start_ahead(pool, [eps_added[0], eps_added[1], eps_added[2], *rstd_ready, hT_lo_ready, wog_ready],
                        [rest_ready[0]])
            rounds(pool, one_round)

        @block.scalar
        def _(act):
            act.dma_start(wmod_sb[:], wmod.rearrange("k (j d) -> k j d", d=D)).then_inc(cond_loaded, 16)
            start_ahead(act, [hT_ready, hT_hi_ready, f_ready, q_sig_ready, *vg_copied, level_copied[6], level_copied[7], cross_copied,
                              onT_ready, h2T_ready, h2_hi_ready, s12_ready, sT_ready, sum_taken],
                        [*hid_ready, rounded])
            act.wait_ge(c_loaded, 16)
            act.activation(c_sig[:], c_sb[:], ACT.Sigmoid).then_inc(setup_act, 1)

            def modulated(out_tile, ps, which, g):
                for b in range(NB):
                    s = slice(b * T, (b + 1) * T)
                    last = act.activation(out_tile[:, s], ps[:, s], ACT.Identity,
                                          scale=modT[:, 2 * which + 1, bass.ds(g * NB + b, 1)],
                                          bias=modT[:, 2 * which, bass.ds(g * NB + b, 1)])
                return last

            def one_round(g, par, front, attention, experts):
                ahead, now, before, older = done(g + 1), done(g), done(g - 1), done(g - 2)
                for step, i in steps(front, attention, experts):
                    if step == "gates":
                        act.wait_ge(setup_pe, PE_SETUP[f"gates{i}"])
                        act.activation(gates[:, 4 * i:4 * i + 4], gates_bank[i][:].rearrange("p (b d) -> p b d", b=4),
                                       ACT.Copy).then_inc(setup_act, 1)
                    elif step == "norm1":
                        act.wait_ge(xn_ps, ahead)
                        if isinstance(g, int) and g == -1:
                            act.wait_ge(setup_dve, DVE_SETUP["mod"])
                        wait(act, vg_ps[1], now)
                        modulated(hT, pA, 0, g + 1).then_inc(hT_ready, 1)
                        act.wait_ge(hT_ready, ahead)
                        act.activation(hT_hi[:], hT[:], ACT.Copy).then_inc(hT_hi_ready, 1)
                        if isinstance(g, int) and g == -1:
                            act.wait_ge(setup_dve, DVE_SETUP["wg12"])
                            act.wait_ge(qkv_loaded, 48)
                            act.activation(w_in_hi[:], w_in[:], ACT.Copy).then_inc(setup_act, 1)
                    elif step == "keys":
                        act.wait_ge(k_ps, ahead)
                        wait(act, cross_ps, now)
                        act.activation(qk[:, 1], pC[:], ACT.Sigmoid)
                        wait(act, carried[1], now)
                        act.activation(f[:], pC[:], ACT.Sigmoid, scale=-1.0).then_inc(f_ready, 1)
                    elif step == "queries":
                        act.wait_ge(q_ps, ahead)
                        act.activation(q_sig[:], pB[:], ACT.Sigmoid).then_inc(q_sig_ready, 1)
                    elif step == "vgate":
                        wait(act, mix_ps, now)
                        wait(act, og_ready, now)
                        vg = (pD, pA)[i][:].rearrange("p (c d) -> p c d", c=2)
                        act.wait_ge(vg_ps[i], ahead)
                        act.activation(gate[:, 2 * i:2 * i + 2], vg[:, :, D:2 * D], ACT.Sigmoid)
                        act.activation(v[:, 2 * i:2 * i + 2], vg[:, :, 0:D], ACT.Copy).then_inc(vg_copied[i], 1)
                    elif step == "level" and i == 6:
                        act.wait_ge(level_ps[6], now)
                        act.wait_ge(level_copied[5], now)
                        ps = pD[:, 0:GROUP // 2].rearrange("p (c t) -> p c t", c=NT)
                        act.activation(at[0:32, :, 32:64], ps[0:32, :, 0:32], ACT.Copy)
                        act.activation(at[64:96, :, 96:128], ps[64:96, :, 32:64], ACT.Copy).then_inc(level_copied[6], 1)
                    elif step == "level" and i == 7:
                        act.wait_ge(level_ps[7], now)
                        ps = pA[:, 0:GROUP // 2].rearrange("p (c t) -> p c t", c=NT)
                        act.activation(at[0:64, :, 64:128], ps[0:64], ACT.Copy).then_inc(level_copied[7], 1)
                    elif step == "cross":
                        act.wait_ge(cross_ps, now)
                        act.activation(ct[:], pB[:, 0:NB * P].rearrange("p (b t) -> p b t", b=NB),
                                       ACT.Copy).then_inc(cross_copied, 1)
                    elif step == "norm2":
                        act.wait_ge(on_ps, now)
                        act.activation(onT[:], pD[:], ACT.Copy).then_inc(onT_ready, 1)
                    elif step == "norm3":
                        act.wait_ge(x2n_ps, now)
                        wait_expert(act, up_ps[HH - 1], E - 1, older)
                        wait(act, h2_lo_ready, older)
                        modulated(h2T[:, par], pB, 1, g).then_inc(h2T_ready, 1)
                        act.wait_ge(h2T_ready, now)
                        act.activation(h2_hi[:, par], h2T[:, par], ACT.Copy).then_inc(h2_hi_ready, 1)
                    elif step == "route":
                        act.wait_ge(lead_ready, now)
                        act.activation(s1[:], lead[:], ACT.Sigmoid)
                        act.activation(s2[:], lead[:], ACT.Sigmoid, scale=-1.0).then_inc(s12_ready, 1)
                    elif step == "turn":
                        act.wait_ge(score_ps, before)
                        wait_expert(act, spread_done, E - 1, older)
                        act.activation(sT[:], pD[0:PARTS], ACT.Copy).then_inc(sT_ready, 1)
                    elif step == "relu":
                        wait_expert(act, weighted_ready, i - 2, before)
                        for j in range(HH):
                            act.wait_ge(up_ps[j], expert_count(i, before))
                            act.activation(hid[:, i % 2, j], hid_ps[j][:], ACT.Relu,
                                           bias=b1T[:, i * HH + j:i * HH + j + 1]).then_inc(hid_ready[j], 1)
                    elif step == "round":
                        act.wait_ge(weighted_ready, expert_count(i, before))
                        wait_expert(act, down_done, i - 2, before)
                        act.activation(w_hid_hi[:, i % 2], weighted[:, i % 2], ACT.Copy).then_inc(rounded, 1)
                    elif step == "final":
                        act.wait_ge(down_done, expert_count(E - 1, before))
                        wait(act, back_ps, older)
                        for b in range(NB):
                            s = slice(b * T, (b + 1) * T)
                            last = act.activation(sumT[:, s], sum_ps[:, s], ACT.Identity,
                                                  scale=gbT[:, bass.ds((g - 1) * NB + b, 1)])
                        last.then_inc(sum_taken, 1)
                if isinstance(g, int) and g == -1:
                    act.wait_ge(w1_loaded, 16)
                    act.activation(w1_hi[:], w1_sb[:], ACT.Copy).then_inc(setup_act, 1)
                    act.wait_ge(b2_loaded, 48)
                    act.activation(b2_hi[:], b2_in[:], ACT.Copy).then_inc(setup_act, 1)
                    act.wait_ge(w2_loaded, 16)
                    act.activation(w2_hi[:], w2_sb[:], ACT.Copy).then_inc(setup_act, 1)

            rounds(act, one_round)

        @block.vector
        def _(dve):
            start_ahead(dve, [*stats_done, *aggr_done, xn_ready, q_ready, sgn_ready, a_ready, og_ready, on_ready,
                              x2_ready, x2n_ready, h2_lo_ready, lead_ready, score_sum, score_hi_ready, score_ready,
                              *level_copied[:6], *carried.values(), *route_step.values(), res_ready],
                        [weighted_ready, rest_ready[1]])
            for s in out_stored:
                dve.sem_inc(s, 16)
            dve.wait_ge(setup_act, ACT_SETUP["cond_sigmoid"])
            dve.tensor_tensor(c_act[:], c_sb[:], c_sig[:], ALU.mult).then_inc(setup_dve, 1)
            dve.wait_ge(setup_pe, PE_SETUP["cond"])
            dve.tensor_copy(cT[:], hid_ps[0][:, 0:B]).then_inc(setup_dve, 1)
            dve.wait_ge(setup_pe, PE_SETUP["wg1"])
            dve.tensor_copy(wg1T[:], sum_ps[:, 0:D]).then_inc(setup_dve, 1)

            def weights_and_gates():
                dve.wait_ge(setup_pe, PE_SETUP["mod"])
                for w in range(4):
                    dve.tensor_scalar(modT[:, w], hid_ps[1][:, w * B:(w + 1) * B], float(w % 2), None, ALU.add)
                dve.tensor_copy(gb_work[0][:], hid_ps[1][:, 4 * B:5 * B])
                dve.tensor_copy(b1T[:], hid_ps[1][:, 5 * B:5 * B + E * HH]).then_inc(setup_dve, 1)
                dve.wait_ge(setup_pe, PE_SETUP["wg12"])
                dve.tensor_copy(w_in[:, 3], hid_ps[0][:, 0:D]).then_inc(setup_dve, 1)
                dve.wait_ge(setup_act, ACT_SETUP["w_in_hi"])
                dve.tensor_tensor(w_in_lo[:], w_in[:], w_in_hi[:].bitcast(F32), ALU.subtract).then_inc(setup_dve, 1)
                dve.wait_ge(setup_pe, PE_SETUP["gate_rows"])
                dve.tensor_copy(ga_work[0][:], spread_ps[0:B, 0:D]).then_inc(setup_dve, 1)
                dve.wait_ge(setup_dve, DVE_SETUP["gate_raw"])
                for raw, sign, mag, _ in (ga_work, gb_work):
                    dve.tensor_scalar(sign[:], raw[:], 0.0, 2.0, ALU.is_ge, ALU.mult)
                    last = dve.scalar_tensor_tensor(mag[:], raw[:], -1.0, raw[:], ALU.mult, ALU.max)
                last.then_inc(setup_dve, 1)
                dve.wait_ge(setup_dve, DVE_SETUP["gate_parts"])
                for _, _, mag, _ in (ga_work, gb_work):
                    last = dve.tensor_scalar(mag[:], mag[:], FLOOR, None, ALU.max)
                last.then_inc(setup_dve, 1)
                dve.wait_ge(setup_dve, DVE_SETUP["gate_floor"])
                for _, sign, mag, signed in (ga_work, gb_work):
                    last = dve.scalar_tensor_tensor(signed[:], sign[:], 1.0, mag[:], ALU.subtract, ALU.mult)
                last.then_inc(setup_dve, 1)
                dve.wait_ge(out_w_loaded, 32)
                dve.tensor_scalar(won[:], wo_sb[:], nw_sb[:, 0:1], None, ALU.mult).then_inc(setup_dve, 1)
                dve.wait_ge(setup_pool, POOL_SETUP["ident"])
                dve.tensor_tensor(pick[:], ident[0:PARTS, 0:E], ident[0:PARTS, 32:32 + E], ALU.add).then_inc(setup_dve, 1)

            def b2_in_parts():
                dve.wait_ge(setup_act, ACT_SETUP["b2_hi"])
                dve.tensor_copy(b2_parts[0:64], b2_in[0:64])
                dve.tensor_tensor(b2_parts[64:PARTS], b2_in[64:PARTS], b2_hi[64:PARTS].bitcast(F32),
                                  ALU.subtract).then_inc(setup_dve, 1)

            def statistics(i, src, now):
                for t in range(NT):
                    last = dve.bn_stats(stat[:, i, t], src[:, t])
                last.then_inc(stats_done[i], 1)
                dve.wait_ge(stats_done[i], now)
                dve.memset(idle[:], 0.0)
                for t in range(NT):
                    last = dve.bn_aggr(mean_var[:, i, t], stat[:, i, t])
                last.then_inc(aggr_done[i], 1)

            def normalized(i, out_tile, src, now):
                dve.wait_ge(rstd_ready[i], now)
                for t in range(NT):
                    last = dve.tensor_scalar(out_tile[:, t], src[:, t], mean_var[:, i, t, 0:1],
                                             rstd[:, i, t:t + 1], ALU.subtract, ALU.mult)
                return last

            def compound(m):
                pair = decay[m][:].rearrange("p (b two) -> p b two", two=2)
                return dve.tensor_tensor(decay[m + 1][:], pair[:, :, 0], pair[:, :, 1], ALU.mult)

            def route(g, par, now, older):
                dve.wait_ge(logit_ps, now)
                lead_view = [P, NT, E]
                logits = pC[:, 0:NT * E].rearrange("p (c e) -> p c e", c=NT)
                dve.tensor_reduce(top1[:], logits, AX.X, ALU.max).then_inc(route_step[1], 1)

                def first_of(top, src, picked, s):
                    dve.wait_ge(route_step[s], now)
                    dve.tensor_tensor(eq[:], src, top[:].unsqueeze(2).to_broadcast(lead_view),
                                      ALU.is_equal).then_inc(route_step[s + 1], 1)
                    dve.wait_ge(route_step[s + 1], now)
                    dve.tensor_tensor(cand[:], eq[:], first_wins[:].rearrange("p (c e) -> p c e", c=NT),
                                      ALU.mult).then_inc(route_step[s + 2], 1)
                    dve.wait_ge(route_step[s + 2], now)
                    dve.tensor_reduce(best[:], cand[:], AX.X, ALU.max).then_inc(route_step[s + 3], 1)
                    dve.wait_ge(route_step[s + 3], now)
                    dve.tensor_tensor(picked[:], cand[:], best[:].unsqueeze(2).to_broadcast(lead_view),
                                      ALU.is_equal).then_inc(route_step[s + 4], 1)

                first_of(top1, logits, pick1, 1)
                dve.wait_ge(route_step[5], now)
                dve.scalar_tensor_tensor(rest[:], pick1[:], LOWEST, logits, ALU.mult, ALU.add).then_inc(route_step[6], 1)
                dve.wait_ge(route_step[6], now)
                dve.tensor_reduce(top2[:], rest[:], AX.X, ALU.max).then_inc(route_step[7], 1)
                dve.wait_ge(route_step[7], now)
                dve.tensor_tensor(lead[:], top1[:], top2[:], ALU.subtract).then_inc(lead_ready, 1)
                first_of(top2, rest[:], pick2, 7)
                dve.wait_ge(s12_ready, now)
                dve.tensor_tensor(part[:], pick1[:], s1[:].unsqueeze(2).to_broadcast(lead_view), ALU.mult)
                dve.wait_ge(route_step[11], now)
                dve.tensor_tensor(pick2[:], pick2[:], s2[:].unsqueeze(2).to_broadcast(lead_view),
                                  ALU.mult).then_inc(route_step[12], 1)
                dve.wait_ge(route_step[12], now)
                dve.tensor_tensor(score[:], part[:], pick2[:], ALU.add).then_inc(score_sum, 1)
                dve.wait_ge(score_sum, now)
                wait(dve, score_ps, older)
                parts = score_parts[:, par]
                dve.tensor_copy(parts[:, :, 0:E], score[:]).then_inc(score_hi_ready, 1)
                dve.tensor_copy(parts[:, :, 64:PARTS], score[:])
                dve.wait_ge(score_hi_ready, now)
                dve.tensor_tensor(parts[:, :, 32:32 + E], score[:], parts[:, :, 0:E].bitcast(F32),
                                  ALU.subtract).then_inc(score_ready, 1)

            def stored_count(g, par):
                if isinstance(g, int):
                    return 16 * ((g - 1) // 2 + 1)
                return 8 * (g + 1) if par == 1 else 8 * g

            def x_count(g, par):
                if isinstance(g, int):
                    return 16 * ((g + 1) // 2 + 1)
                return 8 * (g + 3) if par == 1 else 8 * (g + 2)

            def one_round(g, par, front, attention, experts):
                ahead, now, before, older = done(g + 1), done(g), done(g - 1), done(g - 2)
                first = isinstance(g, int) and g == 0
                for step, i in steps(front, attention, experts):
                    if step == "stats1":
                        dve.wait_ge(x_loaded[1 - par], x_count(g, par))
                        statistics(0, x_sb[:, 1 - par], ahead)
                    elif step == "norm1":
                        normalized(0, xn, x_sb[:, 1 - par], ahead).then_inc(xn_ready, 1)
                        if isinstance(g, int) and g == -1:
                            weights_and_gates()
                    elif step == "queries":
                        dve.wait_ge(q_sig_ready, ahead)
                        wait(dve, level_ps[0], now)
                        dve.tensor_tensor(qraw[:], pB[:], q_sig[:], ALU.mult).then_inc(q_ready, 1)
                    elif step == "decays":
                        dve.wait_ge(f_ready, ahead)
                        dve.tensor_scalar(sgn[:], f[:], 0.5, 2.0, ALU.is_equal, ALU.mult).then_inc(sgn_ready, 1)
                        dve.wait_ge(sgn_ready, ahead)
                        dve.scalar_tensor_tensor(decay[0][:], sgn[:], 1.0, f[:], ALU.subtract, ALU.mult).then_inc(a_ready, 1)
                        dve.wait_ge(q_ready, ahead)
                        dve.wait_ge(a_ready, ahead)
                        wait(dve, cross_ps, now)
                        compound(0)
                        dve.tensor_tensor(qk[:, 0], qraw[:], decay[0][:], ALU.mult).then_inc(carried[1], 1)
                    elif step == "diag":
                        if first:
                            dve.wait_ge(setup_pool, POOL_SETUP["ident"])
                            dve.wait_ge(setup_pool, POOL_SETUP["masks"])
                        dve.wait_ge(level_ps[0], now)
                        wait(dve, mix_ps, before)
                        dve.tensor_tensor(at[:], pB[:].rearrange("p (c t) -> p c t", c=NT),
                                          ident[:].unsqueeze(1).to_broadcast([P, NT, P]), ALU.mult).then_inc(level_copied[0], 1)
                    elif step == "level":
                        m = 1 << (i - 1)
                        dve.wait_ge(level_ps[i], now)
                        dve.wait_ge(carried[i], now)
                        if i < LEVELS:
                            if i <= 5:
                                dve.wait_ge(level_copied[i - 1], now)
                            blocks = GROUP // (2 * m)
                            part_view = halves(m, m, 0, blocks)
                            over = decay[i - 1][:].rearrange("p (b two) -> p two b", two=2)
                            dve.tensor_tensor(part_view, part_view, over.unsqueeze(3).to_broadcast([D, 2, blocks, m]),
                                              ALU.mult).then_inc(carried[i + 1], 1)
                            if i < LEVELS - 1:
                                compound(i)
                        else:
                            over = decay[i - 1][:].rearrange("p (b four) -> p b four", four=4)
                            q2 = qk[:, 0].rearrange("p (b c m) -> p b c m", b=NB, c=4)[:, :, 3]
                            k1 = qk[:, 1].rearrange("p (b c m) -> p b c m", b=NB, c=4)[:, :, 0]
                            dve.tensor_tensor(q2, q2, over[:, :, 2:3].to_broadcast([D, NB, m]), ALU.mult)
                            dve.tensor_tensor(k1, k1, over[:, :, 1:2].to_broadcast([D, NB, m]),
                                              ALU.mult).then_inc(carried[8], 1)
                        if i <= 5:
                            dst = at[:].rearrange("p c (b two m) -> p c b two m", two=2, m=m)[:, :, :, 1]
                            src = LEVEL_BANK[i][:, 0:GROUP // 2].rearrange("p (c b m) -> p c b m", c=NT, m=m)
                            msk = level_mask[:, i - 1].bitcast(I32).rearrange("p (b m) -> p b m", m=m)
                            msk = msk.unsqueeze(1).to_broadcast([P, NT, P // (2 * m), m])
                            dve.copy_predicated(dst, msk, src).then_inc(level_copied[i], 1)
                    elif step == "mix":
                        dve.wait_ge(mix_ps, now)
                        dve.scalar_tensor_tensor(og[:], pC[:].rearrange("p (c d) -> p c d", c=NT), QSCALE, gate[:],
                                                 ALU.mult, ALU.mult).then_inc(og_ready, 1)
                        dve.wait_ge(og_ready, now)
                        statistics(1, og, now)
                    elif step == "norm2":
                        normalized(1, on, og, now).then_inc(on_ready, 1)
                    elif step == "out":
                        dve.wait_ge(out_ps, now)
                        wait(dve, res_ready, older)
                        dve.tensor_tensor(x2[:, par], pA[:].rearrange("p (c d) -> p c d", c=NT), x_sb[:, par],
                                          ALU.add).then_inc(x2_ready, 1)
                        dve.wait_ge(x2_ready, now)
                        statistics(2, x2[:, par], now)
                    elif step == "norm3":
                        normalized(2, x2n, x2[:, par], now).then_inc(x2n_ready, 1)
                    elif step == "h2_lo":
                        dve.wait_ge(h2_hi_ready, now)
                        wait_expert(dve, up_ps[HH - 1], E - 1, older)
                        dve.tensor_tensor(h2_lo[:, par], h2T[:, par], h2_hi[:, par].bitcast(F32),
                                          ALU.subtract).then_inc(h2_lo_ready, 1)
                    elif step == "route":
                        route(g, par, now, older)
                    elif step == "weigh":
                        dve.wait_ge(hid_ready[HH - 1], expert_count(i, before))
                        dve.wait_ge(spread_done, expert_count(i, before))
                        for half in rest_ready:
                            wait_expert(dve, half, i - 2, before)
                        dve.tensor_tensor(weighted[:, i % 2], hid[:, i % 2],
                                          spread_ps[:].unsqueeze(1).to_broadcast([P, HH, GROUP]),
                                          ALU.mult).then_inc(weighted_ready, 1)
                    elif step == "rest":
                        dve.wait_ge(rounded, expert_count(i, before))
                        dve.tensor_tensor(w_hid_lo[:, i % 2, 1], weighted[:, i % 2, 1], w_hid_hi[:, i % 2, 1].bitcast(F32),
                                          ALU.subtract).then_inc(rest_ready[1], 1)
                    elif step == "add":
                        dve.wait_ge(back_ps, before)
                        dve.wait_ge(out_stored[1 - par], stored_count(g, par))
                        dve.tensor_tensor(res[:, 1 - par], spread_ps[:].rearrange("p (c d) -> p c d", c=NT),
                                          x2[:, 1 - par], ALU.add).then_inc(res_ready, 1)
                if first:
                    b2_in_parts()

            rounds(dve, one_round)

        @block.tensor
        def _(pe):
            def mm(o, lhsT, rhs, start=True, stop=True):
                return pe.matmul(o, lhsT, rhs, start=start, stop=stop)

            start_ahead(pe, [xn_ps, q_ps, k_ps, on_ps, out_ps, x2n_ps, logit_ps, score_ps, cross_ps, mix_ps,
                             *vg_ps, *level_ps, back_ps],
                        [*up_ps, spread_done, down_done])
            pe.wait_ge(setup_pool, POOL_SETUP["ident"])
            pe.wait_ge(setup_dve, DVE_SETUP["cond_act"])
            pe.transpose(hid_ps[0][:, 0:B], c_act[:], ident[0:B, 0:B]).then_inc(setup_pe, 1)
            pe.wait_ge(gate_w_loaded, 32)
            pe.transpose(sum_ps[:, 0:D], wg1_sb[:], ident[:]).then_inc(setup_pe, 1)
            pe.wait_ge(b1_loaded, 16)
            pe.transpose(hid_ps[1][:, 5 * B:5 * B + E * HH], b1_rows[:], ident[0:E * HH, 0:E * HH])
            pe.wait_ge(setup_dve, DVE_SETUP["cond_turned"])
            pe.wait_ge(cond_loaded, 16)
            for w, j in enumerate((0, 1, 3, 4, 5)):
                last = mm(hid_ps[1][:, w * B:(w + 1) * B], wmod_sb[:, j], cT[:])
            last.then_inc(setup_pe, 1)
            pe.wait_ge(setup_dve, DVE_SETUP["wg1_turned"])
            mm(hid_ps[0][:, 0:D], wg1T[:], wg2_sb[:]).then_inc(setup_pe, 1)
            mm(spread_ps[0:B, 0:D], cT[:], wmod_sb[:, 2]).then_inc(setup_pe, 1)

            def split_product(o, a_hi, a_lo, b_hi, b_lo):
                mm(o, a_hi, b_hi, stop=False)
                mm(o, a_hi, b_lo, start=False, stop=False)
                return mm(o, a_lo, b_hi, start=False)

            def turn(ps, src):
                for t in range(NT):
                    last = pe.transpose(ps[:, t * P:(t + 1) * P], src[:, t], ident[:])
                return last

            def one_round(g, par, front, attention, experts):
                ahead, now, before, older = done(g + 1), done(g), done(g - 1), done(g - 2)
                first = isinstance(g, int) and g == -1
                for step, i in steps(front, attention, experts):
                    if step == "gates":
                        if i == 0:
                            pe.wait_ge(setup_dve, DVE_SETUP["gates"])
                        for b in range(4):
                            row = ident[0:B, 4 * i + b:4 * i + b + 1].to_broadcast([B, P])
                            last = mm(gates_bank[i][:, b * D:(b + 1) * D], row, ga_rows[:])
                        last.then_inc(setup_pe, 1)
                    elif step == "norm1":
                        pe.wait_ge(xn_ready, ahead)
                        wait(pe, level_copied[7], now)
                        turn(pA, xn).then_inc(xn_ps, 1)
                    elif step == "keys":
                        pe.wait_ge(hT_lo_ready, ahead)
                        if first:
                            pe.wait_ge(setup_dve, DVE_SETUP["w_in_lo"])
                        wait(pe, og_ready, now)
                        split_product(pC[:], w_in_hi[:, 1], w_in_lo[:, 1], hT_hi[:], hT_lo[:]).then_inc(k_ps, 1)
                    elif step == "queries":
                        pe.wait_ge(hT_lo_ready, ahead)
                        if first:
                            pe.wait_ge(setup_dve, DVE_SETUP["w_in_lo"])
                        wait(pe, cross_copied, now)
                        split_product(pB[:], w_in_hi[:, 0], w_in_lo[:, 0], hT_hi[:], hT_lo[:]).then_inc(q_ps, 1)
                    elif step == "vgate":
                        w_hi, w_lo = (w[:, 2:4].rearrange("k j d -> k (j d)") for w in (w_in_hi, w_in_lo))
                        pe.wait_ge(hT_lo_ready, ahead)
                        wait(pe, onT_ready if i == 0 else x2_ready, now)
                        for t in range(2):
                            tok = slice((2 * i + t) * P, (2 * i + t + 1) * P)
                            last = split_product((pD, pA)[i][:, t * 2 * D:(t + 1) * 2 * D], hT_hi[:, tok], hT_lo[:, tok],
                                                 w_hi, w_lo)
                        last.then_inc(vg_ps[i], 1)
                    elif step == "diag":
                        pe.wait_ge(q_ready, now)
                        pe.wait_ge(f_ready, now)
                        wait(pe, h2T_ready, before)
                        for t in range(NT):
                            tok = slice(t * P, (t + 1) * P)
                            last = mm(pB[:, tok], qk[:, 1, tok], qraw[:, tok])
                        last.then_inc(level_ps[0], 1)
                    elif step == "level":
                        m = 1 << (i - 1)
                        pe.wait_ge(carried[i], now)
                        if i == 1:
                            pe.wait_ge(f_ready, now)
                            wait(pe, lead_ready, before)
                        elif i in (2, 3):
                            pe.wait_ge(vg_copied[i - 2], now)
                            if experts and i == 2:
                                pe.wait_ge(sT_ready, before)
                        else:
                            pe.wait_ge(level_copied[i - 4], now)
                        rows = {6: 96, 7: 64}.get(i, P)
                        for t in range(NT):
                            tok = slice(t * P, (t + 1) * P)
                            q_second = qk[:, 0, tok].rearrange("p (b two m) -> p b two m", two=2, m=m)[:, :, 1]
                            last = mm(LEVEL_BANK[i][0:rows, t * P // 2:(t + 1) * P // 2].rearrange("p (b m) -> p b m", m=m),
                                      qk[:, 1, t * P:t * P + rows], q_second)
                        last.then_inc(level_ps[i], 1)
                    elif step == "cross":
                        pe.wait_ge(carried[8], now)
                        pe.wait_ge(level_copied[4], now)
                        for b in range(NB):
                            s, t = slice(2 * b * P, (2 * b + 1) * P), slice((2 * b + 1) * P, (2 * b + 2) * P)
                            last = mm(pB[:, b * P:(b + 1) * P], qk[:, 1, s], qk[:, 0, t])
                        last.then_inc(cross_ps, 1)
                    elif step == "mix":
                        pe.wait_ge(vg_copied[1], now)
                        pe.wait_ge(level_copied[5], now)
                        pe.wait_ge(cross_copied, now)
                        for t in range(NT):
                            o = pC[:, t * D:(t + 1) * D]
                            later = t % TB == 1
                            last = mm(o, at[:, t], v[:, t], stop=not later)
                            if later:
                                last = mm(o, ct[:, t // TB], v[:, t - 1], start=False)
                        last.then_inc(mix_ps, 1)
                    elif step == "norm2":
                        pe.wait_ge(on_ready, now)
                        pe.wait_ge(level_copied[6], now)
                        turn(pD, on).then_inc(on_ps, 1)
                    elif step == "out":
                        pe.wait_ge(onT_ready, now)
                        pe.wait_ge(wog_ready, now)
                        pe.wait_ge(hT_ready, ahead) if front else pe.wait_ge(level_copied[7], now)
                        for t in range(NT):
                            last = mm(pA[:, t * D:(t + 1) * D], onT[:, t * P:(t + 1) * P], wog[:, par, t // TB])
                        last.then_inc(out_ps, 1)
                    elif step == "norm3":
                        pe.wait_ge(x2n_ready, now)
                        if front:
                            pe.wait_ge(q_ready, ahead)
                        turn(pB, x2n).then_inc(x2n_ps, 1)
                    elif step == "route":
                        if isinstance(g, int) and g == 0:
                            pe.wait_ge(router_loaded, 16)
                        pe.wait_ge(h2T_ready, now)
                        pe.wait_ge(f_ready, ahead) if front else pe.wait_ge(og_ready, now)
                        for t in range(NT):
                            last = mm(pC[:, t * E:(t + 1) * E], h2T[:, par, t * P:(t + 1) * P], wr_sb[:])
                        last.then_inc(logit_ps, 1)
                    elif step == "turn":
                        pe.wait_ge(score_ready, before)
                        pe.wait_ge(vg_copied[0], now) if attention else pe.wait_ge(onT_ready, before)
                        for t in range(NT):
                            last = pe.transpose(pD[0:PARTS, t * P:(t + 1) * P], score_parts[:, 1 - par, t].bitcast(F32), ident[:])
                        last.then_inc(score_ps, 1)
                    elif step == "bias":
                        if isinstance(g, int) and g == 1 or not isinstance(g, int):
                            pe.wait_ge(setup_dve, DVE_SETUP["b2_parts"])
                        pe.wait_ge(sT_ready, before)
                        wait(pe, sum_taken, older)
                        mm(sum_ps[:], b2_parts[:], sT[:], stop=False)
                    elif step == "spread":
                        if i >= 1:
                            pe.wait_ge(weighted_ready, expert_count(i - 1, before))
                        else:
                            pe.wait_ge(sT_ready, before)
                            wait(pe, res_ready, older)
                        mm(spread_ps[:], pick[:, i:i + 1].to_broadcast([PARTS, P]), sT[:]).then_inc(spread_done, 1)
                    elif step == "up":
                        if i == 0:
                            pe.wait_ge(h2_lo_ready, before)
                            if isinstance(g, int) and g == 1 or not isinstance(g, int):
                                pe.wait_ge(setup_pool, POOL_SETUP["w1_lo"])
                        x_hi, x_lo = h2_hi[:, 1 - par], h2_lo[:, 1 - par]
                        for j in range(HH):
                            wait_expert(pe, hid_ready[j], i - 1, before)
                            w = slice(j * P, (j + 1) * P)
                            split_product(hid_ps[j][:], w1_hi[:, i, w], w1_lo[:, i, w], x_hi, x_lo).then_inc(up_ps[j], 1)
                    elif step == "down":
                        if i == 0 and (isinstance(g, int) and g == 1 or not isinstance(g, int)):
                            pe.wait_ge(setup_pool, POOL_SETUP["w2_lo"])
                        for half in rest_ready:
                            pe.wait_ge(half, expert_count(i, before))
                        for j in range(HH):
                            mm(sum_ps[:], w2_hi[:, i, j], w_hid_hi[:, i % 2, j], start=False, stop=False)
                            mm(sum_ps[:], w2_hi[:, i, j], w_hid_lo[:, i % 2, j], start=False, stop=False)
                            last = mm(sum_ps[:], w2_lo[:, i, j], w_hid_hi[:, i % 2, j], start=False,
                                      stop=i == E - 1 and j == HH - 1)
                        last.then_inc(down_done, 1)
                    elif step == "back":
                        pe.wait_ge(sum_taken, before)
                        for t in range(NT):
                            last = pe.transpose(spread_ps[:, t * P:(t + 1) * P], sumT[:, t * P:(t + 1) * P], ident[:])
                        last.then_inc(back_ps, 1)
                if isinstance(g, int) and g == 0:
                    pe.wait_ge(setup_act, ACT_SETUP[f"gates{B // 4 - 1}"])

            rounds(pe, one_round)


_INS = ["L0_attn_x", "L0_attn_wq", "L0_attn_wk", "L0_attn_wv", "L0_attn_wo", "L0_attn_wg1", "L0_attn_wg2",
        "L0_attn_norm_w", "L0_ffn_Wg", "L0_ffn_W1", "L0_ffn_b1", "L0_ffn_W2", "L0_ffn_b2", "L0_c", "L0_wmod"]


def kernel(**inputs):
    import numpy as _np
    import concourse.bacc as _bacc
    from concourse import mybir as _mybir
    from concourse.bass_utils import run_bass_kernel_spmd as _run

    nc = _bacc.Bacc("TRN2", target_bir_lowering=False, num_devices=1)
    arrays, args = {}, []
    for name in _INS:
        a = _np.ascontiguousarray(inputs[name])
        arrays[f"in_{name}_dram"] = a
        args.append(nc.dram_tensor(f"in_{name}_dram", a.shape, _mybir.dt.from_np(a.dtype), kind="ExternalInput").ap())
    shape = tuple(inputs["L0_attn_x"].shape)
    out = nc.dram_tensor("out_0_dram", shape, _mybir.dt.float32, kind="ExternalOutput").ap()
    adaln_block_kernel(nc, *args, out)
    r = _run(nc, [arrays], core_ids=[0])
    return r.results[0]["out_0_dram"]
```
